# Optimizing a Trainium2 kernel written in Bass

```python
import numpy as np
import jax
import jax.numpy as jnp

def _softmax(x, axis=-1):
    return jax.nn.softmax(x, axis=axis)

def _gelu(x):
    return jax.nn.gelu(x, approximate=True)

def _silu(x):
    return jax.nn.silu(x)

def _sigmoid(x):
    return jax.nn.sigmoid(x)

def _layernorm(x, axis=-1, eps=1e-05):
    m = jnp.mean(x, axis=axis, keepdims=True)
    v = jnp.var(x, axis=axis, keepdims=True)
    return (x - m) / jnp.sqrt(v + eps)

def _scatter_add(tgt, idx, src, axis=0):
    return tgt.at[idx].add(src)

def _segment_sum(src, seg, n):
    return jax.ops.segment_sum(src, seg, n)
kernel_name = 'mk_conv_preact_d4_conv_nchw2048_r2_3e54d6'

def setup_inputs(seed: int=0):
    np.random.seed(seed)
    _w = jnp.asarray

    def _rec_inputs():
        import jax
        import jax.numpy as jnp
        _gk = jax.random.key(seed)
        x = -7.109e-05 + 0.9999 * jax.random.normal(jax.random.fold_in(_gk, 1), (4, 1024, 32, 32), jnp.float32)
        return x
    x = _rec_inputs()

    def _L0_conv_setup():
        import jax, jax.numpy as jnp
        import numpy as np
        BN_EPS = 1e-05
        key = jax.random.key(seed)
        k1, k2 = jax.random.split(key)
        B, C, H, W = (8, 1024, 32, 32)
        x = jax.random.normal(k1, (B, C, H, W), dtype=jnp.float32)
        cfc_w = jax.random.normal(k2, (C, 3), dtype=jnp.float32) * 0.1
        bn_w = jnp.ones((C,), dtype=jnp.float32)
        bn_b = jnp.zeros((C,), dtype=jnp.float32)
        return {'x': x, 'cfc_w': cfc_w, 'bn_w': bn_w, 'bn_b': bn_b}
    _L0_conv_all = _L0_conv_setup()
    _L0_conv_in = {k: v for k, v in _L0_conv_all.items() if k in ('cfc_w', 'bn_w', 'bn_b')}
    del _L0_conv_all

    def _L1_conv_setup():
        import jax, jax.numpy as jnp
        import numpy as np
        BN_EPS = 1e-05
        key = jax.random.key(seed)
        k1, k2 = jax.random.split(key)
        B, C, H, W = (8, 1024, 32, 32)
        x = jax.random.normal(k1, (B, C, H, W), dtype=jnp.float32)
        cfc_w = jax.random.normal(k2, (C, 3), dtype=jnp.float32) * 0.1
        bn_w = jnp.ones((C,), dtype=jnp.float32)
        bn_b = jnp.zeros((C,), dtype=jnp.float32)
        return {'x': x, 'cfc_w': cfc_w, 'bn_w': bn_w, 'bn_b': bn_b}
    _L1_conv_all = _L1_conv_setup()
    _L1_conv_in = {k: v for k, v in _L1_conv_all.items() if k in ('cfc_w', 'bn_w', 'bn_b')}
    del _L1_conv_all

    def _L2_conv_setup():
        import jax, jax.numpy as jnp
        import numpy as np
        BN_EPS = 1e-05
        key = jax.random.key(seed)
        k1, k2 = jax.random.split(key)
        B, C, H, W = (8, 1024, 32, 32)
        x = jax.random.normal(k1, (B, C, H, W), dtype=jnp.float32)
        cfc_w = jax.random.normal(k2, (C, 3), dtype=jnp.float32) * 0.1
        bn_w = jnp.ones((C,), dtype=jnp.float32)
        bn_b = jnp.zeros((C,), dtype=jnp.float32)
        return {'x': x, 'cfc_w': cfc_w, 'bn_w': bn_w, 'bn_b': bn_b}
    _L2_conv_all = _L2_conv_setup()
    _L2_conv_in = {k: v for k, v in _L2_conv_all.items() if k in ('cfc_w', 'bn_w', 'bn_b')}
    del _L2_conv_all

    def _L3_conv_setup():
        import jax, jax.numpy as jnp
        import numpy as np
        key = jax.random.key(seed)
        k1, k2, k3 = jax.random.split(key, 3)
        N, C, H, W = (4, 1024, 32, 48)
        feature = jax.random.normal(k1, (N, C, H, W), dtype=jnp.float32)
        conv_w = jax.random.normal(k2, (C, C, 1, 9), dtype=jnp.float32) * 0.01
        conv_b = jax.random.normal(k3, (C,), dtype=jnp.float32) * 0.01
        prelu_a = jnp.asarray(0.25, dtype=jnp.float32)
        return {'feature': feature, 'conv_w': conv_w, 'conv_b': conv_b, 'prelu_a': prelu_a}
    _L3_conv_all = _L3_conv_setup()
    _L3_conv_in = {k: v for k, v in _L3_conv_all.items() if k in ('conv_w', 'conv_b', 'prelu_a')}
    del _L3_conv_all
    return {'x': x, 'L0_conv_cfc_w': _L0_conv_in['cfc_w'], 'L0_conv_bn_w': _L0_conv_in['bn_w'], 'L0_conv_bn_b': _L0_conv_in['bn_b'], 'L1_conv_cfc_w': _L1_conv_in['cfc_w'], 'L1_conv_bn_w': _L1_conv_in['bn_w'], 'L1_conv_bn_b': _L1_conv_in['bn_b'], 'L2_conv_cfc_w': _L2_conv_in['cfc_w'], 'L2_conv_bn_w': _L2_conv_in['bn_w'], 'L2_conv_bn_b': _L2_conv_in['bn_b'], 'L3_conv_conv_w': _L3_conv_in['conv_w'], 'L3_conv_conv_b': _L3_conv_in['conv_b'], 'L3_conv_prelu_a': _L3_conv_in['prelu_a']}

def reference(x, L0_conv_cfc_w, L0_conv_bn_w, L0_conv_bn_b, L1_conv_cfc_w, L1_conv_bn_w, L1_conv_bn_b, L2_conv_cfc_w, L2_conv_bn_w, L2_conv_bn_b, L3_conv_conv_w, L3_conv_conv_b, L3_conv_prelu_a):
    import jax
    import jax.numpy as jnp

    def _L0_conv_ref(x, cfc_w, bn_w, bn_b):
        import jax, jax.numpy as jnp
        import numpy as np
        BN_EPS = 1e-05
        b, c, h, w = x.shape
        xf = x.reshape(b, c, h * w)
        mean = jnp.mean(xf, axis=-1)
        mx = jnp.max(xf, axis=-1)
        std = jnp.std(xf, axis=-1, ddof=1)
        u = jnp.stack([mean, mx, std], axis=-1)
        med = jnp.median(u.reshape(b, -1), axis=-1)[:, None, None]
        u = jax.lax.stop_gradient((u - med) ** 3)
        z = jnp.einsum('bck,ck->bc', u, cfc_w)
        z = z / jnp.sqrt(jnp.float32(1.0) + BN_EPS) * bn_w + bn_b
        g = jax.nn.sigmoid(z)
        return x * g[:, :, None, None]

    def _L1_conv_ref(x, cfc_w, bn_w, bn_b):
        import jax, jax.numpy as jnp
        import numpy as np
        BN_EPS = 1e-05
        b, c, h, w = x.shape
        xf = x.reshape(b, c, h * w)
        mean = jnp.mean(xf, axis=-1)
        mx = jnp.max(xf, axis=-1)
        std = jnp.std(xf, axis=-1, ddof=1)
        u = jnp.stack([mean, mx, std], axis=-1)
        med = jnp.median(u.reshape(b, -1), axis=-1)[:, None, None]
        u = jax.lax.stop_gradient((u - med) ** 3)
        z = jnp.einsum('bck,ck->bc', u, cfc_w)
        z = z / jnp.sqrt(jnp.float32(1.0) + BN_EPS) * bn_w + bn_b
        g = jax.nn.sigmoid(z)
        return x * g[:, :, None, None]

    def _L2_conv_ref(x, cfc_w, bn_w, bn_b):
        import jax, jax.numpy as jnp
        import numpy as np
        BN_EPS = 1e-05
        b, c, h, w = x.shape
        xf = x.reshape(b, c, h * w)
        mean = jnp.mean(xf, axis=-1)
        mx = jnp.max(xf, axis=-1)
        std = jnp.std(xf, axis=-1, ddof=1)
        u = jnp.stack([mean, mx, std], axis=-1)
        med = jnp.median(u.reshape(b, -1), axis=-1)[:, None, None]
        u = jax.lax.stop_gradient((u - med) ** 3)
        z = jnp.einsum('bck,ck->bc', u, cfc_w)
        z = z / jnp.sqrt(jnp.float32(1.0) + BN_EPS) * bn_w + bn_b
        g = jax.nn.sigmoid(z)
        return x * g[:, :, None, None]

    def _L3_conv_ref(feature, conv_w, conv_b, prelu_a):
        import jax, jax.numpy as jnp
        import numpy as np
        Wc = conv_w[:, :, 0, 4]

        def step(prev, x_i):
            y = jnp.einsum('oc,nch->noh', Wc, prev) + conv_b[None, :, None]
            y = jnp.where(y >= 0, y, prelu_a * y)
            cur = y + x_i
            return (cur, cur)
        x = jnp.moveaxis(feature, 3, 0)
        _, fwd_rest = jax.lax.scan(step, x[0], x[1:])
        fl = jnp.concatenate([x[0:1], fwd_rest], axis=0)
        _, bwd_rest = jax.lax.scan(step, fl[-1], fl[:-1], reverse=True)
        out = jnp.concatenate([bwd_rest, fl[-1:]], axis=0)
        return jnp.moveaxis(out, 0, 3)

    def _gn(v, G=32, eps=1e-05):
        B_, C_, H_, W_ = v.shape
        g = v.reshape(B_, G, C_ // G, H_, W_)
        m = jnp.mean(g, axis=(2, 3, 4), keepdims=True)
        s = jnp.var(g, axis=(2, 3, 4), keepdims=True)
        return ((g - m) / jnp.sqrt(s + eps)).reshape(v.shape)

    def _ln_c(v, eps=1e-06):
        m = jnp.mean(v, axis=1, keepdims=True)
        s = jnp.var(v, axis=1, keepdims=True)
        return (v - m) / jnp.sqrt(s + eps)

    def _ln_t(v, eps=1e-05):
        m = jnp.mean(v, axis=-1, keepdims=True)
        s = jnp.var(v, axis=-1, keepdims=True)
        return (v - m) / jnp.sqrt(s + eps)

    def _to_tokens(v):
        B_, C_, H_, W_ = v.shape
        return v.reshape(B_, C_, H_ * W_).transpose(0, 2, 1)

    def _from_tokens(t, like):
        B_, C_, H_, W_ = like.shape
        return t.transpose(0, 2, 1).reshape(B_, C_, H_, W_)
    x = x + _L0_conv_ref(_gn(x), L0_conv_cfc_w, L0_conv_bn_w, L0_conv_bn_b)
    x = x + _L1_conv_ref(_gn(x), L1_conv_cfc_w, L1_conv_bn_w, L1_conv_bn_b)
    x = x + _L2_conv_ref(_gn(x), L2_conv_cfc_w, L2_conv_bn_w, L2_conv_bn_b)
    x = x + _L3_conv_ref(_gn(x), L3_conv_conv_w, L3_conv_conv_b, L3_conv_prelu_a)
    return x

_drawn_inputs = setup_inputs


def setup_inputs(seed=0):
    import zlib

    import numpy as np

    out = dict(_drawn_inputs(seed))
    spreads = {'L0_conv_bn_w': (1.0, 0.6),
     'L0_conv_bn_b': (0.0, 0.534),
     'L1_conv_bn_w': (1.0, 0.6),
     'L1_conv_bn_b': (0.0, 0.8),
     'L2_conv_bn_w': (1.0, 0.6),
     'L2_conv_bn_b': (0.0, 0.8)}
    factors = {'L3_conv_conv_b': 8.0}
    for name, (base, spread) in spreads.items():
        noise = np.random.default_rng([zlib.crc32(name.encode()), seed]).standard_normal(out[name].shape)
        drawn = base * np.exp(spread * noise) if base else spread * noise
        out[name] = jnp.asarray(drawn.astype(out[name].dtype))
    for name, factor in factors.items():
        out[name] = (out[name] * factor).astype(out[name].dtype)
    return out
```

```python
import concourse.bass as bass
from concourse import mybir
from contextlib import ExitStack


def gated_norm_and_column_scan_kernel(nc, x_cols, w_t, gate_params, conv_bias, prelu_slope, out_cols):
    fp32 = mybir.dt.float32
    fp32r = mybir.dt.float32r
    bf16 = mybir.dt.bfloat16
    i32 = mybir.dt.int32
    ALU = mybir.AluOpType
    ACT = mybir.ActivationFunctionType
    AX = mybir.AxisListType

    P, CT, COLS, NH = x_cols.shape
    N = 4
    H = NH // N
    C = CT * P
    PIX = H * COLS
    LAYERS = gate_params.shape[1]
    GROUP = C // 32
    NSTAT = 3
    MEDIAN_RANK = C * NSTAT // 2 - 1
    GN_EPS = 1e-5
    BN_DIV = 1.0 / (1.0 + 1e-5) ** 0.5
    HALF = C // 2
    STEPS = 2 * (COLS - 1)

    SEARCH_LO, SEARCH_WIDTH = -8.0, 16.0
    ARY = 8
    T = ARY - 1
    ROUNDS = 9
    BIG = 1e30

    ctx = ExitStack()
    with ctx:
        def sb(name, shape, dt=fp32):
            return ctx.enter_context(nc.sbuf_tensor(name, shape, dt))

        def pb(name, shape, dt=fp32):
            return ctx.enter_context(nc.psum_tensor(name, shape, dt))

        def sem(name):
            return ctx.enter_context(nc.semaphore(name))

        x_sb = sb("x_sb", [P, CT, COLS, NH])
        w_hi = sb("w_hi", [P, CT, C], fp32r)
        w_lo = sb("w_lo", [P, CT, C], fp32r)
        stage = sb("stage", [P, CT * NH])
        ident = sb("ident", [P, P])
        a_scale = sb("a_scale", [P, N, CT])
        a_shift = sb("a_shift", [P, N, CT])
        g_scale = sb("g_scale", [P, N, CT])
        g_shift = sb("g_shift", [P, N, CT])
        bias = sb("bias", [P, CT])
        slope = sb("slope", [P, 1])

        scratch = ExitStack()

        def tmp(name, shape, dt=fp32):
            return scratch.enter_context(nc.sbuf_tensor(name, shape, dt))

        bn_parts = tmp("bn_parts", [P, CT, N, 2, 6])
        mean_var = tmp("mean_var", [P, N, CT, 2])
        stat = tmp("stat", [P, N, NSTAT, CT])
        unit = tmp("unit", [P, N, NSTAT, CT])
        tall = tmp("tall", [P, N, NSTAT, CT])
        cube = tmp("cube", [P, N, NSTAT, CT])
        less = tmp("less", [P, NSTAT * CT, N, T], bf16)
        params = tmp("params", [P, LAYERS, NSTAT + 2, CT])
        group_ones = tmp("group_ones", [P, P])
        ones_bf = tmp("ones_bf", [P, P], bf16)
        ones4 = tmp("ones4", [N, P])
        steps7 = tmp("steps7", [P, T])
        thr = tmp("thr", [P, N, T])
        few = tmp("few", [P, N, T])
        cell = tmp("cell", [P, N])
        lo = tmp("lo", [P, N])
        top8 = tmp("top8", [P, N, 8])
        mid8 = tmp("mid8", [N, 8])
        diag4 = tmp("diag4", [N, N])
        gmean = tmp("gmean", [P, N, CT])
        rstd = tmp("rstd", [P, N, CT])
        var = tmp("var", [P, N, CT])
        t1 = tmp("t1", [P, N, CT])
        t2 = tmp("t2", [P, N, CT])
        gate = tmp("gate", [P, N, CT])
        scratch.close()

        s_hi = sb("s_hi", [P, CT, NH], fp32r)
        s_lo = sb("s_lo", [P, CT, NH], fp32r)
        act_buf = sb("act_buf", [P, HALF])

        ps_prod = [pb(f"ps_prod{c}", [P, HALF]) for c in range(2)]
        ps_turn = [pb(f"ps_turn{r}", [P, 512]) for r in range(2)]
        ps_group = pb("ps_group", [P, 512])
        ps_count = pb("ps_count", [P, 512])
        ps_mid = pb("ps_mid", [P, 512])
        ps_med = pb("ps_med", [P, 512])

        x_loaded = [sem(f"x_loaded{ct}") for ct in range(CT)]
        params_loaded = sem("params_loaded")
        masks_started = sem("masks_started")
        masks_ready = sem("masks_ready")
        w_staged = [sem(f"w_staged{b}") for b in range(2)]
        w_hi_done = sem("w_hi_done")
        w_lo_done = sem("w_lo_done")
        dve_link = sem("dve_link")
        means_asked = sem("means_asked")
        means_given = sem("means_given")
        vars_asked = sem("vars_asked")
        vars_given = sem("vars_given")
        compared = sem("compared")
        counted = sem("counted")
        tops_ready = sem("tops_ready")
        tops_turned = sem("tops_turned")
        median_ready = sem("median_ready")
        median_spread = sem("median_spread")
        logits_ready = sem("logits_ready")
        gates_ready = sem("gates_ready")
        product_done = sem("product_done")
        raw_copied = sem("raw_copied")
        transposed = sem("transposed")
        biased = sem("biased")
        leak_ready = sem("leak_ready")
        column_added = sem("column_added")
        hi_written = sem("hi_written")
        state_ready = sem("state_ready")
        a_state_read = sem("a_state_read")
        norm_scaled = sem("norm_scaled")
        norm_ready = sem("norm_ready")
        x_again = sem("x_again")
        out_scaled = sem("out_scaled")
        out_shifted = sem("out_shifted")
        out_ready = sem("out_ready")
        out_stored = sem("out_stored")

        block = ctx.enter_context(nc.Block())

        W_LOADS = 2 * CT

        def w_half(tile, h):
            return tile[:, h // 2, (h % 2) * HALF:(h % 2 + 1) * HALF]

        def stage_half(h):
            return stage[:, (h % 2) * HALF:(h % 2 + 1) * HALF]

        def over_rows(v, cts=CT):
            return v[:, :, :].rearrange("p n c -> p c n").unsqueeze(3).broadcast_to([P, cts, N, H])

        def column(w, ct0=0, cts=CT):
            return x_sb[:, ct0:ct0 + cts, bass.ds(w, 1), :].rearrange("p c w m -> p c (w m)")

        def by_image(col):
            return col.rearrange("p c (n h) -> p c n h", n=N)

        stage_col = stage[:, :].rearrange("p (c m) -> p c m", c=CT)

        @block.sync
        def _(sp):
            for ct in range(CT):
                sp.dma_start(x_sb[:, ct, :, :], x_cols[:, ct, :, :]).then_inc(x_loaded[ct], 16)
            for h in range(W_LOADS):
                if h >= 2:
                    sp.wait_ge(w_lo_done, h - 1)
                sp.dma_start(stage_half(h), w_half(w_t, h)).then_inc(w_staged[h % 2], 16)
            sp.wait_ge(w_lo_done, W_LOADS)
            sp.dma_start(stage_col, x_cols[:, :, COLS - 1, :]).then_inc(x_again, 16)
            sp.wait_ge(out_ready, 1)
            sp.dma_start(out_cols[COLS - 1], stage[:, :]).then_inc(out_stored, 16)
            with sp.Fori(0, COLS - 1) as b:
                w = COLS - 2 - b
                sp.compute_val(w)
                sp.wait_ge(out_stored, b * 16 + 16)
                sp.dma_start(stage_col, x_cols[:, :, bass.ds(w, 1), :].rearrange("p c w m -> p c (w m)"))\
                    .then_inc(x_again, 16)
                sp.wait_ge(out_ready, b + 2)
                sp.dma_start(out_cols[bass.ds(w, 1)].rearrange("w p m -> (w p) m"), stage[:, :])\
                    .then_inc(out_stored, 16)
            sp.wait_ge(out_stored, COLS * 16)

        @block.gpsimd
        def _(pool):
            pool.memset(ident[:, :], 0.0).then_inc(masks_started, 1)
            pool.memset(group_ones[:, :], 1.0 / GROUP).then_inc(masks_started, 1)
            pool.memset(ones_bf[:, :], 1.0).then_inc(masks_ready, 1)
            pool.memset(ones4[:, :], 1.0).then_inc(masks_ready, 1)
            for j in range(T):
                pool.memset(steps7[:, j:j + 1], float(j + 1)).then_inc(masks_ready, 1)
            pool.wait_ge(masks_started, 2)
            pool.affine_select(out=ident[:, :], in_=ident[:, :], compare_op=ALU.not_equal, fill=1.0,
                               base=0, pattern=[[-1, P]], channel_multiplier=1).then_inc(masks_ready, 1)
            quads = P // GROUP
            by_group = group_ones[:, :].rearrange("p (q c) -> p q c", q=quads)
            pool.affine_select(out=by_group, in_=by_group, compare_op=ALU.is_ge, fill=0.0,
                               base=0, pattern=[[-GROUP, quads], [0, GROUP]], channel_multiplier=1)\
                .then_inc(masks_started, 1)
            pool.wait_ge(masks_started, 3)
            pool.affine_select(out=by_group, in_=by_group, compare_op=ALU.is_ge, fill=0.0,
                               base=GROUP - 1, pattern=[[GROUP, quads], [0, GROUP]], channel_multiplier=-1)\
                .then_inc(masks_ready, 1)
            for h in range(W_LOADS):
                pool.wait_ge(w_hi_done, h + 1)
                pool.tensor_tensor(w_half(w_lo, h), stage_half(h), w_half(w_hi, h).bitcast(fp32), ALU.subtract)\
                    .then_inc(w_lo_done, 1)
        MASKS = 2 + T + 2

        @block.scalar
        def _(act):
            act.dma_start(params[:, :, :, :], gate_params).then_inc(params_loaded, 16)
            act.dma_start(bias[:, :], conv_bias).then_inc(params_loaded, 16)
            act.dma_start(slope[:, :], prelu_slope.partition_broadcast(P)).then_inc(params_loaded, 16)
            for h in range(W_LOADS):
                act.wait_ge(w_staged[h % 2], 16 * (h // 2 + 1))
                act.activation(w_half(w_hi, h), stage_half(h), ACT.Copy).then_inc(w_hi_done, 1)
            for layer in range(LAYERS):
                act.wait_ge(logits_ready, layer + 1)
                act.activation(gate[:, :, :], gate[:, :, :], ACT.Sigmoid).then_inc(gates_ready, 1)
            act.wait_ge(params_loaded, 48)
            with act.Fori(0, STEPS) as i:
                for c in range(2):
                    act.wait_ge(product_done, i * 2 + (c + 1))
                    for r in range(2):
                        half = slice(r * 256, r * 256 + 256)
                        act.wait_ge(column_added, i * 4 + (2 * c + r + 3))
                        act.activation(act_buf[:, half], ps_prod[c][:, half], ACT.Copy).then_inc(raw_copied, 1)
                    for r in range(2):
                        act.wait_ge(transposed, i * 4 + (2 * c + r + 1))
                        for j in range(2):
                            ct = 4 * c + 2 * r + j
                            done = act.activation(act_buf[:, (2 * r + j) * P:(2 * r + j + 1) * P],
                                                  ps_turn[r][:, j * P:(j + 1) * P], ACT.Identity,
                                                  bias=bias[:, ct:ct + 1])
                        done.then_inc(biased, 1)

        @block.tensor
        def _(pe):
            pe.wait_ge(masks_ready, MASKS)
            for layer in range(LAYERS + 1):
                pe.wait_ge(means_asked, layer + 1)
                pe.matmul(ps_group[:, 0:N * CT], group_ones[:, :], stat[:, :, 0, :], start=True, stop=True)\
                    .then_inc(means_given, 1)
                pe.wait_ge(vars_asked, layer + 1)
                pe.matmul(ps_group[:, 0:N * CT], group_ones[:, :], t1[:, :, :].rearrange("p n c -> p (n c)"),
                          start=True, stop=True).then_inc(vars_given, 1)
                if layer == LAYERS:
                    break
                for k in range(ROUNDS):
                    pe.wait_ge(compared, layer * ROUNDS + k + 1)
                    for s in range(NSTAT * CT):
                        last = pe.matmul(ps_count[:, 0:N * T], ones_bf[:, :],
                                         less[:, s, :, :].rearrange("p n t -> p (n t)"),
                                         start=(s == 0), stop=(s == NSTAT * CT - 1))
                    last.then_inc(counted, 1)
                pe.wait_ge(tops_ready, layer + 1)
                for k in range(2):
                    last = pe.matmul(ps_mid[0:N, k * P:(k + 1) * P], top8[:, :, k], ident[:, :],
                                     start=True, stop=True)
                last.then_inc(tops_turned, 1)
                pe.wait_ge(median_ready, layer + 1)
                pe.matmul(ps_med[:, 0:N], ones4[:, :], diag4[:, :], start=True, stop=True)\
                    .then_inc(median_spread, 1)

            pe.wait_ge(w_lo_done, W_LOADS)

            def unit_products(c, k):
                w_cols = slice(c * HALF, (c + 1) * HALF)
                pe.matmul(ps_prod[c][:, :], s_hi[:, k, :], w_hi[:, k, w_cols], start=(k == 0), stop=False)
                pe.matmul(ps_prod[c][:, :], s_hi[:, k, :], w_lo[:, k, w_cols], start=False, stop=False)
                return pe.matmul(ps_prod[c][:, :], s_lo[:, k, :], w_hi[:, k, w_cols],
                                 start=False, stop=(k == CT - 1))

            def turn(r):
                for j in range(2):
                    q = 2 * r + j
                    last = pe.transpose(ps_turn[r][:, j * P:(j + 1) * P], act_buf[:, q * P:(q + 1) * P], ident[:, :])
                last.then_inc(transposed, 1)

            def scan_step(i, first):
                for k in range(4):
                    if k % 2 == 0:
                        pe.wait_ge(state_ready, i * 4 + (k // 2 + 1))
                    unit_products(0, k)
                    if k < 2 and not first:
                        pe.wait_ge(raw_copied, i * 4 + (k - 1))
                        turn(k)
                for k in range(2):
                    unit_products(1, k)
                for k in range(4, CT):
                    if k % 2 == 0:
                        pe.wait_ge(state_ready, i * 4 + (k // 2 + 1))
                    last = unit_products(0, k)
                last.then_inc(product_done, 1)
                for k in range(2, 4):
                    last = unit_products(1, k)
                last.then_inc(a_state_read, 1)
                for k in range(4, CT):
                    last = unit_products(1, k)
                    if k == 4:
                        pe.wait_ge(raw_copied, i * 4 + 1)
                        turn(0)
                    if k == 5:
                        pe.wait_ge(raw_copied, i * 4 + 2)
                        turn(1)
                last.then_inc(product_done, 1)

            scan_step(0, True)
            with pe.Fori(1, STEPS) as i:
                scan_step(i, False)
            for r in range(2):
                pe.wait_ge(raw_copied, 4 * STEPS - 1 + r)
                turn(r)

        @block.vector
        def _(dve):
            links = [0]

            def link(ins):
                links[0] += 1
                ins.then_inc(dve_link, 1)
                dve.wait_ge(dve_link, links[0])

            def rsqrt(out, a, u, v):
                link(dve.tensor_scalar(out.bitcast(i32), a.bitcast(i32), -0.5, float(0x5F3759DF), ALU.mult, ALU.add))
                for _ in range(4):
                    link(dve.tensor_tensor(u, out, out, ALU.mult))
                    link(dve.scalar_tensor_tensor(v, u, -0.5, a, ALU.mult, ALU.mult))
                    link(dve.scalar_tensor_tensor(out, v, 1.5, out, ALU.add, ALU.mult))

            for ct in range(CT):
                dve.wait_ge(x_loaded[ct], 16)
                for n in range(N):
                    for b in range(2):
                        last = dve.bn_stats(bn_parts[:, ct, n, b, :],
                                            x_sb[:, ct, b * 16:(b + 1) * 16, n * H:(n + 1) * H])
                link(last)
                for n in range(N):
                    dve.bn_aggr(mean_var[:, n, ct, :], bn_parts[:, ct, n, :, :].rearrange("p b s -> p (b s)"))
                last = dve.tensor_reduce(stat[:, :, 1, ct],
                                         x_sb[:, ct, :, :].rearrange("p w (n h) -> p n w h", n=N),
                                         AX.XY, ALU.max)
            link(last)
            dve.tensor_copy(stat[:, :, 0, :], mean_var[:, :, :, 0])
            link(dve.tensor_scalar(var[:, :, :], mean_var[:, :, :, 1], PIX / (PIX - 1.0), 1e-30, ALU.mult, ALU.max))
            rsqrt(rstd[:, :, :], var[:, :, :], t1[:, :, :], t2[:, :, :])
            link(dve.tensor_tensor(stat[:, :, 2, :], var[:, :, :], rstd[:, :, :], ALU.mult))
            dve.memset(a_scale[:, :, :], 1.0)
            link(dve.memset(a_shift[:, :, :], 0.0))
            dve.wait_ge(masks_ready, MASKS)
            dve.wait_ge(params_loaded, 48)

            def group_norm(layer):
                link(dve.tensor_tensor(var[:, :, :], stat[:, :, 2, :], stat[:, :, 2, :], ALU.mult))
                dve.wait_ge(means_given, layer + 1)
                link(dve.tensor_copy(gmean[:, :, :].rearrange("p n c -> p (n c)"), ps_group[:, 0:N * CT]))
                link(dve.tensor_tensor(unit[:, :, 0:2, :], stat[:, :, 0:2, :],
                                       gmean[:, :, :].unsqueeze(2).broadcast_to([P, N, 2, CT]), ALU.subtract))
                link(dve.tensor_tensor(t2[:, :, :], unit[:, :, 0, :], unit[:, :, 0, :], ALU.mult))
                dve.scalar_tensor_tensor(t1[:, :, :], var[:, :, :], (PIX - 1.0) / PIX, t2[:, :, :],
                                         ALU.mult, ALU.add).then_inc(vars_asked, 1)
                dve.wait_ge(vars_given, layer + 1)
                link(dve.tensor_scalar(var[:, :, :].rearrange("p n c -> p (n c)"), ps_group[:, 0:N * CT],
                                       GN_EPS, None, ALU.add))
                rsqrt(rstd[:, :, :], var[:, :, :], t1[:, :, :], t2[:, :, :])

            def median(layer):
                values = unit[:, :, :, :].rearrange("p n k c -> p n (k c)")
                link(dve.memset(lo[:, :], SEARCH_LO))
                step = SEARCH_WIDTH
                for k in range(ROUNDS):
                    step /= ARY
                    link(dve.scalar_tensor_tensor(thr[:, :, :], steps7[:, :].unsqueeze(1).broadcast_to([P, N, T]),
                                                  step, lo[:, :].unsqueeze(2).broadcast_to([P, N, T]),
                                                  ALU.mult, ALU.add))
                    dve.tensor_tensor(less[:, :, :, :].rearrange("p s n t -> p n t s"),
                                      values.unsqueeze(2).broadcast_to([P, N, T, NSTAT * CT]),
                                      thr[:, :, :].unsqueeze(3).broadcast_to([P, N, T, NSTAT * CT]),
                                      ALU.is_lt).then_inc(compared, 1)
                    dve.wait_ge(counted, layer * ROUNDS + k + 1)
                    link(dve.tensor_scalar(few[:, :, :].rearrange("p n t -> p (n t)"), ps_count[:, 0:N * T],
                                           float(MEDIAN_RANK), None, ALU.is_le))
                    link(dve.tensor_reduce(cell[:, :], few[:, :, :], AX.X, ALU.add))
                    link(dve.scalar_tensor_tensor(lo[:, :], cell[:, :], step, lo[:, :], ALU.mult, ALU.add))
                spread = tall[:, :, :, :].rearrange("p n k c -> p n (k c)")
                link(dve.tensor_tensor(spread, values, lo[:, :].unsqueeze(2).broadcast_to([P, N, NSTAT * CT]),
                                       ALU.is_lt))
                link(dve.scalar_tensor_tensor(spread, spread, -BIG, values, ALU.mult, ALU.subtract))
                for n in range(N):
                    last = dve.max(top8[:, n, :], spread[:, n, :])
                last.then_inc(tops_ready, 1)
                dve.wait_ge(tops_turned, layer + 1)
                link(dve.max(mid8[:, :], ps_mid[0:N, 0:2 * P]))
                link(dve.tensor_tensor(mid8[:, 2:3], mid8[:, 0:1], mid8[:, 1:2], ALU.add))
                dve.tensor_scalar(diag4[:, :], ident[0:N, 0:N], mid8[:, 2:3], -0.5, ALU.mult, ALU.mult)\
                    .then_inc(median_ready, 1)
                dve.wait_ge(median_spread, layer + 1)

            dve.tensor_copy(t2[:, :, :], stat[:, :, 0, :]).then_inc(means_asked, 1)
            for layer in range(LAYERS):
                group_norm(layer)
                link(dve.tensor_tensor(unit[:, :, 0:2, :], unit[:, :, 0:2, :],
                                       rstd[:, :, :].unsqueeze(2).broadcast_to([P, N, 2, CT]), ALU.mult))
                link(dve.tensor_tensor(unit[:, :, 2, :], stat[:, :, 2, :], rstd[:, :, :], ALU.mult))
                median(layer)
                flat = "p n k c -> p n (k c)"
                link(dve.tensor_tensor(tall[:, :, :, :].rearrange(flat), unit[:, :, :, :].rearrange(flat),
                                       ps_med[:, 0:N].unsqueeze(2).broadcast_to([P, N, NSTAT * CT]), ALU.subtract))
                link(dve.tensor_tensor(cube[:, :, :, :], tall[:, :, :, :], tall[:, :, :, :], ALU.mult))
                link(dve.tensor_tensor(cube[:, :, :, :], cube[:, :, :, :], tall[:, :, :, :], ALU.mult))
                weights = params[:, layer, 0:NSTAT, :].unsqueeze(1).broadcast_to([P, N, NSTAT, CT])
                link(dve.tensor_tensor(cube[:, :, :, :], cube[:, :, :, :], weights, ALU.mult))
                link(dve.tensor_reduce(t1[:, :, :], cube[:, :, :, :].rearrange("p n k c -> p n c k"), AX.X, ALU.add))
                link(dve.scalar_tensor_tensor(t1[:, :, :], t1[:, :, :], BN_DIV,
                                              params[:, layer, NSTAT, :].unsqueeze(1).broadcast_to([P, N, CT]),
                                              ALU.mult, ALU.mult))
                dve.tensor_tensor(gate[:, :, :], t1[:, :, :],
                                  params[:, layer, NSTAT + 1, :].unsqueeze(1).broadcast_to([P, N, CT]),
                                  ALU.add).then_inc(logits_ready, 1)
                dve.wait_ge(gates_ready, layer + 1)
                link(dve.tensor_tensor(tall[:, :, :, :], unit[:, :, :, :],
                                       gate[:, :, :].unsqueeze(2).broadcast_to([P, N, NSTAT, CT]), ALU.mult))
                dve.tensor_tensor(stat[:, :, :, :], stat[:, :, :, :], tall[:, :, :, :], ALU.add)\
                    .then_inc(means_asked, 1)
                dve.wait_ge(means_asked, layer + 2)
                link(dve.tensor_tensor(t1[:, :, :], gate[:, :, :], rstd[:, :, :], ALU.mult))
                link(dve.tensor_tensor(t2[:, :, :], a_scale[:, :, :], t1[:, :, :], ALU.mult))
                link(dve.tensor_tensor(a_scale[:, :, :], a_scale[:, :, :], t2[:, :, :], ALU.add))
                link(dve.tensor_tensor(t2[:, :, :], a_shift[:, :, :], gmean[:, :, :], ALU.subtract))
                link(dve.tensor_tensor(t2[:, :, :], t2[:, :, :], t1[:, :, :], ALU.mult))
                link(dve.tensor_tensor(a_shift[:, :, :], a_shift[:, :, :], t2[:, :, :], ALU.add))
            group_norm(LAYERS)
            link(dve.tensor_tensor(t1[:, :, :], a_shift[:, :, :], gmean[:, :, :], ALU.subtract))
            dve.tensor_tensor(g_scale[:, :, :], a_scale[:, :, :], rstd[:, :, :], ALU.mult)
            link(dve.tensor_tensor(g_shift[:, :, :], t1[:, :, :], rstd[:, :, :], ALU.mult))

            def norm_column(w, count):
                dve.tensor_tensor(by_image(column(w)), by_image(column(w)), over_rows(g_scale), ALU.mult)\
                    .then_inc(norm_scaled, 1)
                dve.wait_ge(norm_scaled, count + 1)
                dve.tensor_tensor(by_image(column(w)), by_image(column(w)), over_rows(g_shift), ALU.add)\
                    .then_inc(norm_ready, 1)

            def split_state(w, ct0, nth):
                col = column(w, ct0, 2)
                hi, low = s_hi[:, ct0:ct0 + 2, :], s_lo[:, ct0:ct0 + 2, :]
                dve.tensor_scalar(hi, col, 1.0, None, ALU.mult).then_inc(hi_written, 1)
                dve.wait_ge(hi_written, nth)
                dve.tensor_tensor(low, col, hi.bitcast(fp32), ALU.subtract).then_inc(state_ready, 1)

            def scan_step(i, w):
                for c in range(2):
                    for r in range(2):
                        ct0 = 4 * c + 2 * r
                        nth = i * 4 + (2 * c + r + 5)
                        dve.wait_ge(biased, i * 4 + (2 * c + r + 1))
                        y = act_buf[:, r * 256:(r + 1) * 256].rearrange("p (c m) -> p c m", c=2)
                        col = column(w, ct0, 2)
                        dve.scalar_tensor_tensor(col, y, 0.0, col, ALU.max, ALU.add)
                        dve.tensor_scalar(y, y, 0.0, slope[:, 0:1], ALU.min, ALU.mult).then_inc(leak_ready, 1)
                        dve.wait_ge(leak_ready, nth - 4)
                        dve.tensor_tensor(col, col, y, ALU.add).then_inc(column_added, 1)
                        dve.wait_ge(column_added, nth)
                        if c == 0 and r == 0:
                            dve.wait_ge(a_state_read, i + 1)
                        split_state(w, ct0, nth)

            def output_column(w, nth):
                dve.wait_ge(x_again, nth * 16)
                dve.tensor_tensor(by_image(stage_col), by_image(stage_col), over_rows(a_scale), ALU.mult)\
                    .then_inc(out_scaled, 1)
                dve.wait_ge(out_scaled, nth)
                dve.tensor_tensor(by_image(stage_col), by_image(stage_col), over_rows(a_shift), ALU.add)\
                    .then_inc(out_shifted, 1)
                dve.wait_ge(out_shifted, nth)
                dve.tensor_tensor(stage_col, stage_col, column(w), ALU.add).then_inc(out_ready, 1)

            dve.tensor_tensor(by_image(column(0)), by_image(column(0)), over_rows(g_scale), ALU.mult)\
                .then_inc(norm_scaled, 1)
            dve.wait_ge(norm_scaled, 1)
            for q in range(4):
                pair = by_image(column(0, 2 * q, 2))
                shift = g_shift[:, :, 2 * q:2 * q + 2].rearrange("p n c -> p c n").unsqueeze(3)
                dve.tensor_tensor(pair, pair, shift.broadcast_to([P, 2, N, H]), ALU.add).then_inc(column_added, 1)
                dve.wait_ge(column_added, q + 1)
                split_state(0, 2 * q, q + 1)
            norm_column(1, 1)
            with dve.Fori(0, COLS - 2) as i:
                dve.wait_ge(norm_ready, i + 1)
                scan_step(i, i + 1)
                norm_column(i + 2, i + 2)
            dve.wait_ge(norm_ready, COLS - 1)
            scan_step(COLS - 2, COLS - 1)
            output_column(COLS - 1, 1)
            with dve.Fori(0, COLS - 1) as b:
                w = COLS - 2 - b
                dve.compute_val(w)
                scan_step(b + (COLS - 1), w)
                output_column(w, b + 2)


def kernel(x, L0_conv_cfc_w, L0_conv_bn_w, L0_conv_bn_b, L1_conv_cfc_w, L1_conv_bn_w, L1_conv_bn_b,
           L2_conv_cfc_w, L2_conv_bn_w, L2_conv_bn_b, L3_conv_conv_w, L3_conv_conv_b, L3_conv_prelu_a):
    import numpy as np
    import concourse.bacc as bacc
    from concourse.bass_utils import run_bass_kernel_spmd

    x = np.asarray(x)
    n, c, h, w = x.shape
    p, ct = 128, c // 128
    x_cols = np.ascontiguousarray(x.reshape(n, ct, p, h, w).transpose(2, 1, 4, 0, 3)).reshape(p, ct, w, n * h)
    w_t = np.ascontiguousarray(np.asarray(L3_conv_conv_w)[:, :, 0, 4].T.reshape(ct, p, c).transpose(1, 0, 2))
    by_tile = lambda v: np.asarray(v).reshape(ct, p, -1).transpose(1, 2, 0)
    gates = np.ascontiguousarray(np.stack([
        np.concatenate([by_tile(a), by_tile(b), by_tile(d)], axis=1)
        for a, b, d in ((L0_conv_cfc_w, L0_conv_bn_w, L0_conv_bn_b),
                        (L1_conv_cfc_w, L1_conv_bn_w, L1_conv_bn_b),
                        (L2_conv_cfc_w, L2_conv_bn_w, L2_conv_bn_b))], axis=1))
    bias = np.ascontiguousarray(by_tile(L3_conv_conv_b)[:, 0, :])
    slope = np.asarray(L3_conv_prelu_a).reshape(1)

    nc = bacc.Bacc("TRN2", target_bir_lowering=False, num_devices=1)
    arrays = {"x_cols": x_cols, "w_t": w_t, "gates": gates, "conv_bias": bias, "prelu_slope": slope}
    args = [nc.dram_tensor(name, a.shape, mybir.dt.from_np(a.dtype), kind="ExternalInput").ap()
            for name, a in arrays.items()]
    out = nc.dram_tensor("out_cols", (w, p, ct * n * h), mybir.dt.float32, kind="ExternalOutput").ap()
    gated_norm_and_column_scan_kernel(nc, *args, out)
    got = run_bass_kernel_spmd(nc, [arrays], core_ids=[0]).results[0]["out_cols"]
    return np.ascontiguousarray(got.reshape(w, p, ct, n, h).transpose(3, 2, 1, 4, 0)).reshape(n, c, h, w)
```

```python
import concourse.bass as bass
from concourse import mybir
from contextlib import ExitStack


def gated_norm_and_column_scan_kernel(nc, x_cols, w_t, gate_params, conv_bias, prelu_slope, out_cols):
    fp32 = mybir.dt.float32
    fp32r = mybir.dt.float32r
    bf16 = mybir.dt.bfloat16
    i32 = mybir.dt.int32
    ALU = mybir.AluOpType
    ACT = mybir.ActivationFunctionType
    AX = mybir.AxisListType

    P, CT, COLS, NH = x_cols.shape
    N = 4
    H = NH // N
    C = CT * P
    PIX = H * COLS
    LAYERS = gate_params.shape[1]
    GROUP = C // 32
    NSTAT = 3
    MEDIAN_RANK = C * NSTAT // 2 - 1
    GN_EPS = 1e-5
    BN_DIV = 1.0 / (1.0 + 1e-5) ** 0.5
    HALF = C // 2
    STEPS = 2 * (COLS - 1)

    SEARCH_LO, SEARCH_WIDTH = -8.0, 16.0
    ARY = 8
    T = ARY - 1
    ROUNDS = 9
    VALUES = NSTAT * CT
    BIG = 1e30

    ctx = ExitStack()
    with ctx:
        def sb(name, shape, dt=fp32):
            return ctx.enter_context(nc.sbuf_tensor(name, shape, dt))

        def pb(name, shape, dt=fp32):
            return ctx.enter_context(nc.psum_tensor(name, shape, dt))

        def sem(name):
            return ctx.enter_context(nc.semaphore(name))

        x_sb = sb("x_sb", [P, CT, COLS, NH])
        w_hi = sb("w_hi", [P, CT, C], fp32r)
        w_lo = sb("w_lo", [P, CT, C], fp32r)
        stage = sb("stage", [P, CT * NH])
        ident = sb("ident", [P, P])
        a_scale = sb("a_scale", [P, N, CT])
        a_shift = sb("a_shift", [P, N, CT])
        g_scale = sb("g_scale", [P, N, CT])
        g_shift = sb("g_shift", [P, N, CT])
        bias = sb("bias", [P, CT])
        neg_bias = sb("neg_bias", [P, CT])
        slope = sb("slope", [P, 1])
        neg_slope = sb("neg_slope", [P, 1])

        scratch = ExitStack()

        def tmp(name, shape, dt=fp32):
            return scratch.enter_context(nc.sbuf_tensor(name, shape, dt))

        bn_parts = tmp("bn_parts", [P, CT, N, 2, 6])
        half_max = tmp("half_max", [P, 2, N, CT])
        mean_div = tmp("mean_div", [P, N, CT])
        mean_var = tmp("mean_var", [P, N, CT, 2])
        stat = tmp("stat", [P, N, NSTAT, CT])
        unit = tmp("unit", [P, N, NSTAT, CT])
        tall = tmp("tall", [P, N, NSTAT, CT])
        cube = tmp("cube", [P, N, NSTAT + 1, CT])
        less = tmp("less", [P, NSTAT * CT, N, T], bf16)
        params = tmp("params", [P, LAYERS, NSTAT + 2, CT])
        group_ones = tmp("group_ones", [P, P])
        ones_bf = tmp("ones_bf", [P, P], bf16)
        ones4 = tmp("ones4", [N, P])
        steps7 = tmp("steps7", [P, T])
        thr = tmp("thr", [P, N, T])
        few = tmp("few", [P, N, T])
        base = tmp("base", [P, N, T])
        edge = tmp("edge", [P, N])
        cell = tmp("cell", [P, N])
        lo = tmp("lo", [P, N])
        top8 = tmp("top8", [P, N, 8])
        mid8 = tmp("mid8", [N, 8])
        diag4 = tmp("diag4", [N, N])
        gmean = tmp("gmean", [P, N, CT])
        rstd = tmp("rstd", [P, N, CT])
        var = tmp("var", [P, N, CT])
        t1 = tmp("t1", [P, N, CT])
        t2 = tmp("t2", [P, N, CT])
        gate = tmp("gate", [P, N, CT])
        scratch.close()

        s_hi = sb("s_hi", [P, CT, NH], fp32r)
        s_lo = sb("s_lo", [P, CT, NH], fp32r)
        act_buf = sb("act_buf", [P, HALF])

        ps_prods = pb("ps_prods", [P, 2 * HALF])
        ps_prod = [ps_prods[:, c * HALF:(c + 1) * HALF] for c in range(2)]
        ps_turns = pb("ps_turns", [P, 2 * 512])
        ps_turn = [ps_turns[:, r * 512:(r + 1) * 512] for r in range(2)]
        ps_group = pb("ps_group", [P, 512])
        ps_count = pb("ps_count", [P, 512])
        ps_mid = pb("ps_mid", [P, 512])
        ps_med = pb("ps_med", [P, 512])
        ps_var = ps_med

        x_loaded = [[sem(f"x_loaded{ct}_{b}") for b in range(2)] for ct in range(CT)]
        act_summed = sem("act_summed")
        act_shift_done = sem("act_shift_done")
        params_loaded = sem("params_loaded")
        folded = sem("folded")
        masks_started = sem("masks_started")
        masks_ready = sem("masks_ready")
        w_staged = [sem(f"w_staged{b}") for b in range(2)]
        w_hi_done = sem("w_hi_done")
        w_lo_done = sem("w_lo_done")
        dve_link = sem("dve_link")
        means_asked = sem("means_asked")
        means_given = sem("means_given")
        vars_asked = sem("vars_asked")
        vars_given = sem("vars_given")
        compared = sem("compared")
        counted = sem("counted")
        tops_ready = sem("tops_ready")
        tops_turned = sem("tops_turned")
        median_ready = sem("median_ready")
        median_spread = sem("median_spread")
        logits_ready = sem("logits_ready")
        gates_ready = sem("gates_ready")
        product_done = sem("product_done")
        raw_copied = sem("raw_copied")
        transposed = sem("transposed")
        biased = sem("biased")
        negated = sem("negated")
        above_added = sem("above_added")
        column_added = sem("column_added")
        hi_written = sem("hi_written")
        state_ready = sem("state_ready")
        a_state_read = sem("a_state_read")
        norm_scaled = sem("norm_scaled")
        norm_ready = sem("norm_ready")
        x_again = sem("x_again")
        out_scaled = sem("out_scaled")
        out_shifted = sem("out_shifted")
        out_ready = sem("out_ready")
        out_stored = sem("out_stored")

        block = ctx.enter_context(nc.Block())

        W_LOADS = 2 * CT

        def w_half(tile, h):
            return tile[:, h // 2, (h % 2) * HALF:(h % 2 + 1) * HALF]

        def stage_half(h):
            return stage[:, (h % 2) * HALF:(h % 2 + 1) * HALF]

        def over_rows(v, cts=CT):
            return v[:, :, :].rearrange("p n c -> p c n").unsqueeze(3).broadcast_to([P, cts, N, H])

        def column(w, ct0=0, cts=CT):
            return x_sb[:, ct0:ct0 + cts, bass.ds(w, 1), :].rearrange("p c w m -> p c (w m)")

        def by_image(col):
            return col.rearrange("p c (n h) -> p c n h", n=N)

        waste = [t[:, :].rearrange("p (w h) -> p w h", w=COLS) for t in (ps_prods, ps_turns)]

        def vector_images(ct):
            return 2 - ct % 2

        act_passes = sum(2 * (N - vector_images(ct)) for ct in range(CT))

        stage_col = stage[:, :].rearrange("p (c m) -> p c m", c=CT)

        @block.sync
        def _(sp):
            for ct in range(CT):
                for b in range(2):
                    cols = slice(b * COLS // 2, (b + 1) * COLS // 2)
                    sp.dma_start(x_sb[:, ct, cols, :], x_cols[:, ct, cols, :]).then_inc(x_loaded[ct][b], 16)
            for h in range(W_LOADS):
                if h >= 2:
                    sp.wait_ge(w_lo_done, h - 1)
                sp.dma_start(stage_half(h), w_half(w_t, h)).then_inc(w_staged[h % 2], 16)
            sp.wait_ge(w_lo_done, W_LOADS)
            sp.dma_start(stage_col, x_cols[:, :, COLS - 1, :]).then_inc(x_again, 16)
            with sp.Fori(0, COLS - 1) as b:
                w = COLS - 1 - b
                sp.compute_val(w)
                sp.wait_ge(out_ready, b + 1)
                sp.dma_start(stage_col, x_cols[:, :, bass.ds(w - 1, 1), :].rearrange("p c w m -> p c (w m)"))\
                    .then_inc(x_again, 16)
                sp.dma_start(out_cols[bass.ds(w, 1)].rearrange("w p (c m) -> p c (w m)", c=CT), column(w))\
                    .then_inc(out_stored, 16)
            sp.wait_ge(out_ready, COLS)
            sp.dma_start(out_cols[0].rearrange("p (c m) -> p c m", c=CT), column(0)).then_inc(out_stored, 16)
            sp.wait_ge(out_stored, COLS * 16)

        @block.gpsimd
        def _(pool):
            pool.memset(ident[:, :], 0.0).then_inc(masks_started, 1)
            pool.memset(group_ones[:, :], 1.0 / GROUP).then_inc(masks_started, 1)
            pool.memset(ones_bf[:, :], 1.0).then_inc(masks_ready, 1)
            pool.memset(ones4[:, :], 1.0).then_inc(masks_ready, 1)
            for j in range(T):
                pool.memset(steps7[:, j:j + 1], float(j + 1)).then_inc(masks_ready, 1)
            pool.wait_ge(masks_started, 2)
            pool.affine_select(out=ident[:, :], in_=ident[:, :], compare_op=ALU.not_equal, fill=1.0,
                               base=0, pattern=[[-1, P]], channel_multiplier=1).then_inc(masks_ready, 1)
            quads = P // GROUP
            by_group = group_ones[:, :].rearrange("p (q c) -> p q c", q=quads)
            pool.affine_select(out=by_group, in_=by_group, compare_op=ALU.is_ge, fill=0.0,
                               base=0, pattern=[[-GROUP, quads], [0, GROUP]], channel_multiplier=1)\
                .then_inc(masks_started, 1)
            pool.wait_ge(masks_started, 3)
            pool.affine_select(out=by_group, in_=by_group, compare_op=ALU.is_ge, fill=0.0,
                               base=GROUP - 1, pattern=[[GROUP, quads], [0, GROUP]], channel_multiplier=-1)\
                .then_inc(masks_ready, 1)
            pool.wait_ge(params_loaded, 48)
            pool.tensor_scalar(neg_bias[:, :], bias[:, :], -1.0, 0.0, ALU.mult, ALU.add).then_inc(folded, 1)
            pool.tensor_scalar(neg_slope[:, :], slope[:, :], -1.0, 0.0, ALU.mult, ALU.add).then_inc(folded, 1)
            for layer in range(LAYERS):
                pool.tensor_scalar(params[:, layer, NSTAT, :], params[:, layer, NSTAT, :], BN_DIV, 0.0,
                                   ALU.mult, ALU.add).then_inc(folded, 1)
                pool.wait_ge(folded, 2 * layer + 3)
                pool.tensor_tensor(params[:, layer, 0:NSTAT, :], params[:, layer, 0:NSTAT, :],
                                   params[:, layer, NSTAT, :].unsqueeze(1).broadcast_to([P, NSTAT, CT]),
                                   ALU.mult).then_inc(folded, 1)
            for h in range(W_LOADS):
                pool.wait_ge(w_hi_done, h + 1)
                pool.tensor_tensor(w_half(w_lo, h), stage_half(h), w_half(w_hi, h).bitcast(fp32), ALU.subtract)\
                    .then_inc(w_lo_done, 1)
        MASKS = 2 + T + 2

        @block.scalar
        def _(act):
            act.dma_start(params[:, :, :, :], gate_params).then_inc(params_loaded, 16)
            act.dma_start(bias[:, :], conv_bias).then_inc(params_loaded, 16)
            act.dma_start(slope[:, :], prelu_slope.partition_broadcast(P)).then_inc(params_loaded, 16)
            passes = 0

            def plane_sum(n, ct, func, out, **affine):
                nonlocal passes
                if passes >= 2:
                    act.wait_ge(act_summed, passes - 1)
                act.activation(waste[passes % 2], x_sb[:, ct, :, n * H:(n + 1) * H], func,
                               accum_out=out, **affine).then_inc(act_summed, 1)
                passes += 1

            for ct in range(CT):
                for b in range(2):
                    act.wait_ge(x_loaded[ct][b], 16)
                mine = range(vector_images(ct), N)
                for n in mine:
                    plane_sum(n, ct, ACT.Copy, mean_var[:, n, ct, 0:1], scale=1.0 / PIX)
                act.wait_ge(act_summed, passes)
                act.activation(mean_div[:, mine[0]:N, ct], mean_var[:, mine[0]:N, ct, 0], ACT.Copy,
                               scale=-PIX ** -0.5).then_inc(act_shift_done, 1)
                act.wait_ge(act_shift_done, ct + 1)
                for n in mine:
                    plane_sum(n, ct, ACT.Square, mean_var[:, n, ct, 1:2], scale=PIX ** -0.5,
                              bias=mean_div[:, n, ct:ct + 1])
            for h in range(W_LOADS):
                act.wait_ge(w_staged[h % 2], 16 * (h // 2 + 1))
                act.activation(w_half(w_hi, h), stage_half(h), ACT.Copy).then_inc(w_hi_done, 1)
            for layer in range(LAYERS):
                act.wait_ge(logits_ready, layer + 1)
                act.activation(gate[:, :, :], gate[:, :, :], ACT.Sigmoid).then_inc(gates_ready, 1)
            act.wait_ge(params_loaded, 48)
            act.wait_ge(folded, 2)
            with act.Fori(0, STEPS) as i:
                for c in range(2):
                    act.wait_ge(product_done, i * 2 + (c + 1))
                    for r in range(2):
                        half = slice(r * 256, r * 256 + 256)
                        act.wait_ge(column_added, i * 4 + (2 * c + r + 3))
                        act.activation(act_buf[:, half], ps_prod[c][:, half], ACT.Copy).then_inc(raw_copied, 1)
                    for r in range(2):
                        act.wait_ge(transposed, i * 4 + (2 * c + r + 1))
                        for j in range(2):
                            ct = 4 * c + 2 * r + j
                            last = act.activation(act_buf[:, (2 * r + j) * P:(2 * r + j + 1) * P],
                                                  ps_turn[r][:, j * P:(j + 1) * P], ACT.Identity,
                                                  bias=bias[:, ct:ct + 1])
                        last.then_inc(biased, 1)
                        act.wait_ge(biased, i * 4 + (2 * c + r + 1))
                        for j in range(2):
                            ct = 4 * c + 2 * r + j
                            tile = ps_turn[r][:, j * P:(j + 1) * P]
                            last = act.activation(tile, tile, ACT.Relu, bias=neg_bias[:, ct:ct + 1], scale=-1.0)
                        last.then_inc(negated, 1)

        @block.tensor
        def _(pe):
            pe.wait_ge(masks_ready, MASKS)
            for layer in range(LAYERS + 1):
                pe.wait_ge(means_asked, layer + 1)
                pe.matmul(ps_group[:, 0:N * CT], group_ones[:, :], stat[:, :, 0, :], start=True, stop=True)\
                    .then_inc(means_given, 1)
                pe.wait_ge(vars_asked, layer + 1)
                pe.matmul(ps_var[:, 0:N * CT], group_ones[:, :], t1[:, :, :].rearrange("p n c -> p (n c)"),
                          start=True, stop=True).then_inc(vars_given, 1)
                if layer == LAYERS:
                    break
                for k in range(ROUNDS):
                    for s in range(VALUES):
                        if s % (VALUES // 2) == 0:
                            pe.wait_ge(compared, (layer * ROUNDS + k) * 2 + 1 + s // (VALUES // 2))
                        last = pe.matmul(ps_count[:, 0:N * T], ones_bf[:, :],
                                         less[:, s, :, :].rearrange("p n t -> p (n t)"),
                                         start=(s == 0), stop=(s == VALUES - 1))
                    last.then_inc(counted, 1)
                pe.wait_ge(tops_ready, layer + 1)
                for k in range(2):
                    last = pe.matmul(ps_mid[0:N, k * P:(k + 1) * P], top8[:, :, k], ident[:, :],
                                     start=True, stop=True)
                last.then_inc(tops_turned, 1)
                pe.wait_ge(median_ready, layer + 1)
                pe.matmul(ps_med[:, 0:N], ones4[:, :], diag4[:, :], start=True, stop=True)\
                    .then_inc(median_spread, 1)

            pe.wait_ge(w_lo_done, W_LOADS)

            def unit_products(c, k):
                w_cols = slice(c * HALF, (c + 1) * HALF)
                pe.matmul(ps_prod[c], s_hi[:, k, :], w_hi[:, k, w_cols], start=(k == 0), stop=False)
                pe.matmul(ps_prod[c], s_hi[:, k, :], w_lo[:, k, w_cols], start=False, stop=False)
                return pe.matmul(ps_prod[c], s_lo[:, k, :], w_hi[:, k, w_cols],
                                 start=False, stop=(k == CT - 1))

            def turn(r):
                for j in range(2):
                    q = 2 * r + j
                    last = pe.transpose(ps_turn[r][:, j * P:(j + 1) * P], act_buf[:, q * P:(q + 1) * P], ident[:, :])
                last.then_inc(transposed, 1)

            def scan_step(i, first):
                for k in range(4):
                    if k % 2 == 0:
                        pe.wait_ge(state_ready, i * 4 + (k // 2 + 1))
                    unit_products(0, k)
                    if k < 2 and not first:
                        pe.wait_ge(raw_copied, i * 4 + (k - 1))
                        turn(k)
                for k in range(2):
                    unit_products(1, k)
                for k in range(4, CT):
                    if k % 2 == 0:
                        pe.wait_ge(state_ready, i * 4 + (k // 2 + 1))
                    last = unit_products(0, k)
                last.then_inc(product_done, 1)
                for k in range(2, CT):
                    last = unit_products(1, k)
                    if k == 3:
                        last.then_inc(a_state_read, 1)
                    if k < 4:
                        pe.wait_ge(raw_copied, i * 4 + (k - 1))
                        turn(k - 2)
                last.then_inc(product_done, 1)

            scan_step(0, True)
            with pe.Fori(1, STEPS) as i:
                scan_step(i, False)
            for r in range(2):
                pe.wait_ge(raw_copied, 4 * STEPS - 1 + r)
                turn(r)

        @block.vector
        def _(dve):
            links = [0]

            def link(ins):
                links[0] += 1
                ins.then_inc(dve_link, 1)
                dve.wait_ge(dve_link, links[0])

            def rsqrt(out, a, u, v):
                link(dve.tensor_scalar(out.bitcast(i32), a.bitcast(i32), -0.5, float(0x5F3759DF), ALU.mult, ALU.add))
                for _ in range(3):
                    link(dve.tensor_tensor(u, out, out, ALU.mult))
                    link(dve.scalar_tensor_tensor(v, u, -0.5, a, ALU.mult, ALU.mult))
                    link(dve.scalar_tensor_tensor(out, v, 1.5, out, ALU.add, ALU.mult))

            for ct in range(CT):
                for b in range(2):
                    dve.wait_ge(x_loaded[ct][b], 16)
                    cols = slice(b * COLS // 2, (b + 1) * COLS // 2)
                    for n in range(vector_images(ct)):
                        last = dve.bn_stats(bn_parts[:, ct, n, b, :], x_sb[:, ct, cols, n * H:(n + 1) * H])
                    if b == 1:
                        link(last)
                        for n in range(vector_images(ct)):
                            dve.bn_aggr(mean_var[:, n, ct, :], bn_parts[:, ct, n, :, :].rearrange("p b s -> p (b s)"))
                    last = dve.tensor_reduce(half_max[:, b, :, ct],
                                             x_sb[:, ct, cols, :].rearrange("p w (n h) -> p n w h", n=N),
                                             AX.XY, ALU.max)
            link(last)
            dve.tensor_tensor(stat[:, :, 1, :], half_max[:, 0, :, :], half_max[:, 1, :, :], ALU.max)
            dve.wait_ge(act_summed, act_passes)
            dve.tensor_copy(stat[:, :, 0, :], mean_var[:, :, :, 0])
            link(dve.tensor_scalar(var[:, :, :], mean_var[:, :, :, 1], PIX / (PIX - 1.0), 1e-30, ALU.mult, ALU.max))
            rsqrt(rstd[:, :, :], var[:, :, :], t1[:, :, :], t2[:, :, :])
            link(dve.tensor_tensor(stat[:, :, 2, :], var[:, :, :], rstd[:, :, :], ALU.mult))
            dve.memset(a_scale[:, :, :], 1.0)
            link(dve.memset(a_shift[:, :, :], 0.0))
            dve.wait_ge(masks_ready, MASKS)
            dve.wait_ge(params_loaded, 48)
            dve.wait_ge(folded, 2 * LAYERS + 2)

            def group_norm(layer):
                dve.tensor_tensor(var[:, :, :], stat[:, :, 2, :], stat[:, :, 2, :], ALU.mult)
                dve.wait_ge(means_given, layer + 1)
                means = ps_group[:, 0:N * CT].rearrange("p (n c) -> p n c", n=N)
                link(dve.tensor_tensor(unit[:, :, 0:2, :], stat[:, :, 0:2, :],
                                       means.unsqueeze(2).broadcast_to([P, N, 2, CT]), ALU.subtract))
                link(dve.tensor_tensor(t2[:, :, :], unit[:, :, 0, :], unit[:, :, 0, :], ALU.mult))
                dve.scalar_tensor_tensor(t1[:, :, :], var[:, :, :], (PIX - 1.0) / PIX, t2[:, :, :],
                                         ALU.mult, ALU.add).then_inc(vars_asked, 1)
                dve.tensor_copy(gmean[:, :, :], means)
                dve.wait_ge(vars_given, layer + 1)
                link(dve.tensor_scalar(var[:, :, :].rearrange("p n c -> p (n c)"), ps_var[:, 0:N * CT],
                                       GN_EPS, None, ALU.add))
                rsqrt(rstd[:, :, :], var[:, :, :], t1[:, :, :], t2[:, :, :])

            def median(layer):
                values = unit[:, :, :, :].rearrange("p n k c -> p n (k c)")
                own = lambda v: v[:, :].unsqueeze(2).broadcast_to([P, N, T])
                nth = steps7[:, :].unsqueeze(1).broadcast_to([P, N, T])
                step = SEARCH_WIDTH / ARY
                dve.memset(lo[:, :], SEARCH_LO)
                link(dve.tensor_scalar(thr[:, :, :], nth, step, SEARCH_LO, ALU.mult, ALU.add))
                for k in range(ROUNDS):
                    for part in range(2):
                        vals = slice(part * VALUES // 2, (part + 1) * VALUES // 2)
                        dve.tensor_tensor(less[:, vals, :, :].rearrange("p s n t -> p n t s"),
                                          values[:, :, vals].unsqueeze(2).broadcast_to([P, N, T, VALUES // 2]),
                                          thr[:, :, :].unsqueeze(3).broadcast_to([P, N, T, VALUES // 2]),
                                          ALU.is_lt).then_inc(compared, 1)
                    if k > 0:
                        link(dve.scalar_tensor_tensor(lo[:, :], cell[:, :], step * ARY, lo[:, :], ALU.mult, ALU.add))
                    if k < ROUNDS - 1:
                        link(dve.scalar_tensor_tensor(base[:, :, :], nth, step / ARY, own(lo), ALU.mult, ALU.add))
                    dve.wait_ge(counted, layer * ROUNDS + k + 1)
                    link(dve.tensor_scalar(few[:, :, :].rearrange("p n t -> p (n t)"), ps_count[:, 0:N * T],
                                           float(MEDIAN_RANK), None, ALU.is_le))
                    link(dve.tensor_reduce(cell[:, :], few[:, :, :], AX.X, ALU.add))
                    if k < ROUNDS - 1:
                        link(dve.scalar_tensor_tensor(thr[:, :, :], own(cell), step, base[:, :, :],
                                                      ALU.mult, ALU.add))
                        step /= ARY
                link(dve.scalar_tensor_tensor(lo[:, :], cell[:, :], step, lo[:, :], ALU.mult, ALU.add))
                link(dve.tensor_scalar(edge[:, :], lo[:, :], -1.0, None, ALU.mult))
                link(dve.tensor_tensor(edge[:, :], edge[:, :], lo[:, :], ALU.max))
                link(dve.scalar_tensor_tensor(lo[:, :], edge[:, :], -(2.0 ** -22), lo[:, :], ALU.mult, ALU.add))
                spread = tall[:, :, :, :].rearrange("p n k c -> p n (k c)")
                link(dve.tensor_tensor(spread, values, lo[:, :].unsqueeze(2).broadcast_to([P, N, VALUES]),
                                       ALU.is_lt))
                link(dve.scalar_tensor_tensor(spread, spread, -BIG, values, ALU.mult, ALU.subtract))
                for n in range(N):
                    last = dve.max(top8[:, n, :], spread[:, n, :])
                last.then_inc(tops_ready, 1)
                dve.wait_ge(tops_turned, layer + 1)
                link(dve.max(mid8[:, :], ps_mid[0:N, 0:2 * P]))
                link(dve.tensor_tensor(mid8[:, 2:3], mid8[:, 0:1], mid8[:, 1:2], ALU.add))
                dve.tensor_scalar(diag4[:, :], ident[0:N, 0:N], mid8[:, 2:3], -0.5, ALU.mult, ALU.mult)\
                    .then_inc(median_ready, 1)
                dve.wait_ge(median_spread, layer + 1)

            dve.tensor_copy(t2[:, :, :], stat[:, :, 0, :]).then_inc(means_asked, 1)
            for layer in range(LAYERS):
                dve.tensor_copy(cube[:, :, NSTAT, :],
                                params[:, layer, NSTAT + 1, :].unsqueeze(1).broadcast_to([P, N, CT]))
                group_norm(layer)
                link(dve.tensor_tensor(unit[:, :, 0:2, :], unit[:, :, 0:2, :],
                                       rstd[:, :, :].unsqueeze(2).broadcast_to([P, N, 2, CT]), ALU.mult))
                link(dve.tensor_tensor(unit[:, :, 2, :], stat[:, :, 2, :], rstd[:, :, :], ALU.mult))
                median(layer)
                link(dve.tensor_tensor(tall[:, :, :, :].rearrange("p n k c -> p n (k c)"),
                                       unit[:, :, :, :].rearrange("p n k c -> p n (k c)"),
                                       ps_med[:, 0:N].unsqueeze(2).broadcast_to([P, N, VALUES]), ALU.subtract))
                dve.tensor_tensor(cube[:, :, 0:NSTAT, :], tall[:, :, :, :], tall[:, :, :, :], ALU.mult)
                weights = params[:, layer, 0:NSTAT, :].unsqueeze(1).broadcast_to([P, N, NSTAT, CT])
                link(dve.tensor_tensor(tall[:, :, :, :], tall[:, :, :, :], weights, ALU.mult))
                link(dve.tensor_tensor(cube[:, :, 0:NSTAT, :], cube[:, :, 0:NSTAT, :], tall[:, :, :, :], ALU.mult))
                dve.tensor_reduce(gate[:, :, :], cube[:, :, :, :].rearrange("p n k c -> p n c k"), AX.X, ALU.add)\
                    .then_inc(logits_ready, 1)
                dve.wait_ge(gates_ready, layer + 1)
                link(dve.tensor_tensor(tall[:, :, :, :], unit[:, :, :, :],
                                       gate[:, :, :].unsqueeze(2).broadcast_to([P, N, NSTAT, CT]), ALU.mult))
                dve.tensor_tensor(stat[:, :, :, :], stat[:, :, :, :], tall[:, :, :, :], ALU.add)\
                    .then_inc(means_asked, 1)
                dve.wait_ge(means_asked, layer + 2)
                link(dve.tensor_tensor(t1[:, :, :], gate[:, :, :], rstd[:, :, :], ALU.mult))
                link(dve.tensor_tensor(t2[:, :, :], a_scale[:, :, :], t1[:, :, :], ALU.mult))
                link(dve.tensor_tensor(a_scale[:, :, :], a_scale[:, :, :], t2[:, :, :], ALU.add))
                link(dve.tensor_tensor(t2[:, :, :], a_shift[:, :, :], gmean[:, :, :], ALU.subtract))
                link(dve.tensor_tensor(t2[:, :, :], t2[:, :, :], t1[:, :, :], ALU.mult))
                link(dve.tensor_tensor(a_shift[:, :, :], a_shift[:, :, :], t2[:, :, :], ALU.add))
            group_norm(LAYERS)
            link(dve.tensor_tensor(t1[:, :, :], a_shift[:, :, :], gmean[:, :, :], ALU.subtract))
            dve.tensor_tensor(g_scale[:, :, :], a_scale[:, :, :], rstd[:, :, :], ALU.mult)
            link(dve.tensor_tensor(g_shift[:, :, :], t1[:, :, :], rstd[:, :, :], ALU.mult))

            def norm_column(w, count):
                dve.tensor_tensor(by_image(column(w)), by_image(column(w)), over_rows(g_scale), ALU.mult)\
                    .then_inc(norm_scaled, 1)
                dve.wait_ge(norm_scaled, count + 1)
                dve.tensor_tensor(by_image(column(w)), by_image(column(w)), over_rows(g_shift), ALU.add)\
                    .then_inc(norm_ready, 1)

            def split_state(w, ct0, nth):
                col = column(w, ct0, 2)
                hi, low = s_hi[:, ct0:ct0 + 2, :], s_lo[:, ct0:ct0 + 2, :]
                dve.tensor_scalar(hi, col, 1.0, None, ALU.mult).then_inc(hi_written, 1)
                dve.wait_ge(hi_written, nth)
                dve.tensor_tensor(low, col, hi.bitcast(fp32), ALU.subtract).then_inc(state_ready, 1)

            def scan_step(i, w):
                for c in range(2):
                    for r in range(2):
                        ct0 = 4 * c + 2 * r
                        nth = i * 4 + (2 * c + r + 5)
                        dve.wait_ge(biased, i * 4 + (2 * c + r + 1))
                        y = act_buf[:, r * 256:(r + 1) * 256].rearrange("p (c m) -> p c m", c=2)
                        col = column(w, ct0, 2)
                        below = ps_turn[r][:, 0:256].rearrange("p (c m) -> p c m", c=2)
                        dve.scalar_tensor_tensor(col, y, 0.0, col, ALU.max, ALU.add).then_inc(above_added, 1)
                        dve.wait_ge(above_added, i * 4 + (2 * c + r + 1))
                        dve.wait_ge(negated, i * 4 + (2 * c + r + 1))
                        dve.scalar_tensor_tensor(col, below, neg_slope[:, 0:1], col, ALU.mult, ALU.add)\
                            .then_inc(column_added, 1)
                        dve.wait_ge(column_added, nth)
                        if c == 0 and r == 0:
                            dve.wait_ge(a_state_read, i + 1)
                        split_state(w, ct0, nth)

            def gated_column(nth):
                dve.wait_ge(x_again, nth * 16)
                dve.tensor_tensor(by_image(stage_col), by_image(stage_col), over_rows(a_scale), ALU.mult)\
                    .then_inc(out_scaled, 1)
                dve.wait_ge(out_scaled, nth)
                dve.tensor_tensor(by_image(stage_col), by_image(stage_col), over_rows(a_shift), ALU.add)\
                    .then_inc(out_shifted, 1)

            def output_column(w, nth, pairs):
                dve.wait_ge(state_ready, pairs)
                dve.wait_ge(out_shifted, nth)
                dve.tensor_tensor(column(w), column(w), stage_col, ALU.add).then_inc(out_ready, 1)

            dve.tensor_tensor(by_image(column(0)), by_image(column(0)), over_rows(g_scale), ALU.mult)\
                .then_inc(norm_scaled, 1)
            dve.wait_ge(norm_scaled, 1)
            for q in range(4):
                pair = by_image(column(0, 2 * q, 2))
                shift = g_shift[:, :, 2 * q:2 * q + 2].rearrange("p n c -> p c n").unsqueeze(3)
                dve.tensor_tensor(pair, pair, shift.broadcast_to([P, 2, N, H]), ALU.add).then_inc(column_added, 1)
                dve.wait_ge(column_added, q + 1)
                split_state(0, 2 * q, q + 1)
            norm_column(1, 1)
            with dve.Fori(0, COLS - 2) as i:
                dve.wait_ge(norm_ready, i + 1)
                scan_step(i, i + 1)
                norm_column(i + 2, i + 2)
            dve.wait_ge(norm_ready, COLS - 1)
            scan_step(COLS - 2, COLS - 1)
            gated_column(1)
            output_column(COLS - 1, 1, 4 * COLS)
            with dve.Fori(0, COLS - 2) as b:
                w = COLS - 2 - b
                dve.compute_val(w)
                scan_step(b + (COLS - 1), w)
                gated_column(b + 2)
                output_column(w, b + 2, (b + COLS) * 4 + 4)
            gated_column(COLS)
            scan_step(STEPS - 1, 0)
            output_column(0, COLS, 4 * STEPS + 4)


def kernel(x, L0_conv_cfc_w, L0_conv_bn_w, L0_conv_bn_b, L1_conv_cfc_w, L1_conv_bn_w, L1_conv_bn_b,
           L2_conv_cfc_w, L2_conv_bn_w, L2_conv_bn_b, L3_conv_conv_w, L3_conv_conv_b, L3_conv_prelu_a):
    import numpy as np
    import concourse.bacc as bacc
    from concourse.bass_utils import run_bass_kernel_spmd

    x = np.asarray(x)
    n, c, h, w = x.shape
    p, ct = 128, c // 128
    x_cols = np.ascontiguousarray(x.reshape(n, ct, p, h, w).transpose(2, 1, 4, 0, 3)).reshape(p, ct, w, n * h)
    w_t = np.ascontiguousarray(np.asarray(L3_conv_conv_w)[:, :, 0, 4].T.reshape(ct, p, c).transpose(1, 0, 2))
    by_tile = lambda v: np.asarray(v).reshape(ct, p, -1).transpose(1, 2, 0)
    gates = np.ascontiguousarray(np.stack([
        np.concatenate([by_tile(a), by_tile(b), by_tile(d)], axis=1)
        for a, b, d in ((L0_conv_cfc_w, L0_conv_bn_w, L0_conv_bn_b),
                        (L1_conv_cfc_w, L1_conv_bn_w, L1_conv_bn_b),
                        (L2_conv_cfc_w, L2_conv_bn_w, L2_conv_bn_b))], axis=1))
    bias = np.ascontiguousarray(by_tile(L3_conv_conv_b)[:, 0, :])
    slope = np.asarray(L3_conv_prelu_a).reshape(1)

    nc = bacc.Bacc("TRN2", target_bir_lowering=False, num_devices=1)
    arrays = {"x_cols": x_cols, "w_t": w_t, "gates": gates, "conv_bias": bias, "prelu_slope": slope}
    args = [nc.dram_tensor(name, a.shape, mybir.dt.from_np(a.dtype), kind="ExternalInput").ap()
            for name, a in arrays.items()]
    out = nc.dram_tensor("out_cols", (w, p, ct * n * h), mybir.dt.float32, kind="ExternalOutput").ap()
    gated_norm_and_column_scan_kernel(nc, *args, out)
    got = run_bass_kernel_spmd(nc, [arrays], core_ids=[0]).results[0]["out_cols"]
    return np.ascontiguousarray(got.reshape(w, p, ct, n, h).transpose(3, 2, 1, 4, 0)).reshape(n, c, h, w)
```

```python
import concourse.bass as bass
from concourse import mybir
from contextlib import ExitStack
import itertools


def gated_norm_and_column_scan_kernel(nc, x_cols, w_t, gate_params, conv_bias, prelu_slope, out_cols):
    fp32 = mybir.dt.float32
    fp32r = mybir.dt.float32r
    bf16 = mybir.dt.bfloat16
    i32 = mybir.dt.int32
    ALU = mybir.AluOpType
    ACT = mybir.ActivationFunctionType
    AX = mybir.AxisListType

    P, CT, COLS, NH = x_cols.shape
    N = 4
    H = NH // N
    C = CT * P
    PIX = H * COLS
    LAYERS = gate_params.shape[1]
    GROUP = C // 32
    NSTAT = 3
    MEDIAN_RANK = C * NSTAT // 2 - 1
    GN_EPS = 1e-5
    BN_DIV = 1.0 / (1.0 + 1e-5) ** 0.5
    HALF = C // 2
    STEPS = 2 * (COLS - 1)

    SEARCH_LO, SEARCH_WIDTH = -149 / 256, 2.0
    ARY = 8
    ROUNDS = 8
    VALUES = NSTAT * CT
    PARTS = [0, 11, 19]
    BIG = 1e30
    WARM_UPS = 11

    ctx = ExitStack()
    with ctx:
        def sb(name, shape, dt=fp32):
            return ctx.enter_context(nc.sbuf_tensor(name, shape, dt))

        def pb(name, shape, dt=fp32):
            return ctx.enter_context(nc.psum_tensor(name, shape, dt))

        def sem(name):
            return ctx.enter_context(nc.semaphore(name))

        x_sb = sb("x_sb", [P, CT, COLS, NH])
        w_hi = sb("w_hi", [P, CT, C], fp32r)
        w_lo = sb("w_lo", [P, CT, C], fp32r)
        stage = sb("stage", [P, CT * NH])
        ident = sb("ident", [P, P])
        a_scale = sb("a_scale", [P, N, CT])
        a_shift = sb("a_shift", [P, N, CT])
        g_scale = sb("g_scale", [P, N, CT])
        g_shift = sb("g_shift", [P, N, CT])
        bias = sb("bias", [P, CT])
        neg_bias = sb("neg_bias", [P, CT])
        slope = sb("slope", [P, 1])
        neg_slope = sb("neg_slope", [P, 1])

        scratch = ExitStack()

        def tmp(name, shape, dt=fp32):
            return scratch.enter_context(nc.sbuf_tensor(name, shape, dt))

        bn_parts = tmp("bn_parts", [P, CT, N, 2, 6])
        half_max = tmp("half_max", [P, 2, N, CT])
        mean_div = tmp("mean_div", [P, N, CT])
        mean_var = tmp("mean_var", [P, N, CT, 2])
        stat = tmp("stat", [P, N, NSTAT, CT])
        unit = tmp("unit", [P, N, NSTAT, CT])
        tall = tmp("tall", [P, N, NSTAT, CT])
        cube = tmp("cube", [P, N, NSTAT + 1, CT])
        less = tmp("less", [P, VALUES * N * ARY], bf16)
        params = tmp("params", [P, LAYERS, NSTAT + 2, CT])
        group_ones = tmp("group_ones", [P, P])
        ones_bf = tmp("ones_bf", [P, P], bf16)
        ones8 = tmp("ones8", [2 * N, P])
        ticks = tmp("ticks", [P, ARY])
        thr = tmp("thr", [P, N * ARY])
        base = tmp("base", [P, N * ARY])
        few = tmp("few", [P, 2, N * ARY])
        cell = tmp("cell", [P, 2, N])
        lo = tmp("lo", [P, N])
        floors = tmp("floors", [P, 2, N])
        spread = tmp("spread", [P, 2, N, VALUES])
        tops = tmp("tops", [P, 2 * N])
        middle = tmp("middle", [2 * N, 1])
        fold = tmp("fold", [2 * N, N])
        halves = tmp("halves", [2 * N, N])
        rstd = tmp("rstd", [P, 2, N, CT])
        var = tmp("var", [P, 2, N, CT])
        t1 = tmp("t1", [P, 2, N, CT])
        t2 = tmp("t2", [P, 2, N, CT])
        gate = tmp("gate", [P, N, CT])
        grow = tmp("grow", [P, N, CT])
        pull = tmp("pull", [P, N, CT])
        scaled = tmp("scaled", [P, N, CT])
        scratch.close()

        s_hi = sb("s_hi", [P, CT, NH], fp32r)
        s_lo = sb("s_lo", [P, CT, NH], fp32r)
        act_buf = sb("act_buf", [P, HALF])

        ps_prods = pb("ps_prods", [P, 2 * HALF])
        ps_prod = [ps_prods[:, c * HALF:(c + 1) * HALF] for c in range(2)]
        ps_turns = pb("ps_turns", [P, 2 * 512])
        ps_turn = [ps_turns[:, r * 512:(r + 1) * 512] for r in range(2)]
        ps_below = pb("ps_below", [P, 2 * 512])
        ps_group = pb("ps_group", [P, 512])
        ps_count = ps_below[:, 0:512]
        ps_mid = ps_below[:, 512:1024]
        ps_med = pb("ps_med", [P, 512])
        ps_var = ps_med

        x_loaded = [[sem(f"x_loaded{ct}_{b}") for b in range(2)] for ct in range(CT)]
        act_summed = sem("act_summed")
        act_shift_done = sem("act_shift_done")
        params_loaded = sem("params_loaded")
        folded = sem("folded")
        masks_started = sem("masks_started")
        masks_ready = sem("masks_ready")
        w_staged = [sem(f"w_staged{b}") for b in range(2)]
        w_hi_done = sem("w_hi_done")
        w_lo_done = sem("w_lo_done")
        dve_link = sem("dve_link")
        means_asked = sem("means_asked")
        means_given = sem("means_given")
        vars_asked = sem("vars_asked")
        vars_given = sem("vars_given")
        compared = sem("compared")
        counted = sem("counted")
        tops_ready = sem("tops_ready")
        tops_turned = sem("tops_turned")
        median_ready = sem("median_ready")
        median_spread = sem("median_spread")
        logits_ready = sem("logits_ready")
        gates_ready = sem("gates_ready")
        product_done = sem("product_done")
        raw_copied = sem("raw_copied")
        transposed = sem("transposed")
        biased = sem("biased")
        negated = sem("negated")
        above_added = sem("above_added")
        column_added = sem("column_added")
        hi_written = sem("hi_written")
        state_ready = sem("state_ready")
        a_state_read = sem("a_state_read")
        norm_scaled = sem("norm_scaled")
        norm_ready = sem("norm_ready")
        x_again = sem("x_again")
        gates_folded = sem("gates_folded")
        spare_scaled = sem("spare_scaled")
        spare_ready = sem("spare_ready")
        out_scaled = sem("out_scaled")
        out_shifted = sem("out_shifted")
        out_ready = sem("out_ready")
        out_stored = sem("out_stored")

        block = ctx.enter_context(nc.Block())

        W_LOADS = 2 * CT

        def w_half(tile, h):
            return tile[:, h // 2, (h % 2) * HALF:(h % 2 + 1) * HALF]

        def stage_half(h):
            return stage[:, (h % 2) * HALF:(h % 2 + 1) * HALF]

        def over_rows(v, cts=CT):
            return v[:, :, :].rearrange("p n c -> p c n").unsqueeze(3).broadcast_to([P, cts, N, H])

        def column(w, ct0=0, cts=CT):
            return x_sb[:, ct0:ct0 + cts, bass.ds(w, 1), :].rearrange("p c w m -> p c (w m)")

        def by_image(col):
            return col.rearrange("p c (n h) -> p c n h", n=N)

        waste = [t[:, :].rearrange("p (w h) -> p w h", w=COLS) for t in (ps_prods, ps_turns)]

        def vector_images(ct):
            return 2 - ct % 2

        act_passes = 1 + sum(2 * (N - vector_images(ct)) for ct in range(CT))

        def round_marks(k):
            return ARY if k == ROUNDS - 1 else ARY - 1

        stage_col = stage[:, :].rearrange("p (c m) -> p c m", c=CT)

        spare_col = column(COLS - 1)

        @block.sync
        def _(sp):
            for ct in range(CT):
                for b in range(2):
                    cols = slice(b * COLS // 2, (b + 1) * COLS // 2)
                    sp.dma_start(x_sb[:, ct, cols, :], x_cols[:, ct, cols, :]).then_inc(x_loaded[ct][b], 16)
            for h in range(W_LOADS):
                if h >= 2:
                    sp.wait_ge(w_lo_done, h - 1)
                sp.dma_start(stage_half(h), w_half(w_t, h)).then_inc(w_staged[h % 2], 16)
            sp.wait_ge(w_lo_done, W_LOADS)
            sp.dma_start(stage_col, x_cols[:, :, COLS - 1, :]).then_inc(x_again, 16)
            with sp.Fori(0, COLS - 2) as b:
                w = COLS - 1 - b
                sp.compute_val(w)
                sp.wait_ge(out_ready, b + 1)
                sp.dma_start(stage_col, x_cols[:, :, bass.ds(w - 1, 1), :].rearrange("p c w m -> p c (w m)"))\
                    .then_inc(x_again, 16)
                sp.dma_start(out_cols[bass.ds(w, 1)].rearrange("w p (c m) -> p c (w m)", c=CT), column(w))\
                    .then_inc(out_stored, 16)
            sp.wait_ge(out_stored, (COLS - 2) * 16)
            sp.dma_start(spare_col, x_cols[:, :, 0, :]).then_inc(x_again, 16)
            sp.wait_ge(out_ready, COLS - 1)
            sp.dma_start(out_cols[1].rearrange("p (c m) -> p c m", c=CT), column(1)).then_inc(out_stored, 16)
            for c in range(2):
                half = slice(4 * c, 4 * c + 4)
                sp.wait_ge(out_ready, COLS + c)
                sp.dma_start(out_cols[0].rearrange("p (c m) -> p c m", c=CT)[:, half, :], column(0, 4 * c, 4))\
                    .then_inc(out_stored, 16)
            sp.wait_ge(out_stored, (COLS + 1) * 16)

        @block.gpsimd
        def _(pool):
            pool.memset(ident[:, :], 0.0).then_inc(masks_started, 1)
            pool.memset(group_ones[:, :], 1.0 / GROUP).then_inc(masks_started, 1)
            pool.memset(ones_bf[:, :], 1.0).then_inc(masks_ready, 1)
            pool.memset(ones8[:, :], 1.0).then_inc(masks_ready, 1)
            for j in range(ARY):
                pool.memset(ticks[:, j:j + 1], float(j + 1)).then_inc(masks_ready, 1)
            pool.wait_ge(masks_started, 2)
            pool.affine_select(out=ident[:, :], in_=ident[:, :], compare_op=ALU.not_equal, fill=1.0,
                               base=0, pattern=[[-1, P]], channel_multiplier=1).then_inc(masks_ready, 1)
            quads = P // GROUP
            by_group = group_ones[:, :].rearrange("p (q c) -> p q c", q=quads)
            pool.affine_select(out=by_group, in_=by_group, compare_op=ALU.is_ge, fill=0.0,
                               base=0, pattern=[[-GROUP, quads], [0, GROUP]], channel_multiplier=1)\
                .then_inc(masks_started, 1)
            pool.wait_ge(masks_started, 3)
            pool.affine_select(out=by_group, in_=by_group, compare_op=ALU.is_ge, fill=0.0,
                               base=GROUP - 1, pattern=[[GROUP, quads], [0, GROUP]], channel_multiplier=-1)\
                .then_inc(masks_ready, 1)
            pool.wait_ge(params_loaded, 48)
            pool.tensor_scalar(neg_bias[:, :], bias[:, :], -1.0, 0.0, ALU.mult, ALU.add).then_inc(folded, 1)
            pool.tensor_scalar(neg_slope[:, :], slope[:, :], -1.0, 0.0, ALU.mult, ALU.add).then_inc(folded, 1)
            for layer in range(LAYERS):
                pool.tensor_scalar(params[:, layer, NSTAT, :], params[:, layer, NSTAT, :], BN_DIV, 0.0,
                                   ALU.mult, ALU.add).then_inc(folded, 1)
                pool.wait_ge(folded, 2 * layer + 3)
                pool.tensor_tensor(params[:, layer, 0:NSTAT, :], params[:, layer, 0:NSTAT, :],
                                   params[:, layer, NSTAT, :].unsqueeze(1).broadcast_to([P, NSTAT, CT]),
                                   ALU.mult).then_inc(folded, 1)
            for h in range(W_LOADS):
                pool.wait_ge(w_hi_done, h + 1)
                pool.tensor_tensor(w_half(w_lo, h), stage_half(h), w_half(w_hi, h).bitcast(fp32), ALU.subtract)\
                    .then_inc(w_lo_done, 1)
            pool.wait_ge(gates_folded, 1)
            pool.wait_ge(x_again, COLS * 16)
            pool.tensor_tensor(by_image(spare_col), by_image(spare_col), over_rows(a_scale), ALU.mult)\
                .then_inc(spare_scaled, 1)
            pool.wait_ge(spare_scaled, 1)
            pool.tensor_tensor(by_image(spare_col), by_image(spare_col), over_rows(a_shift), ALU.add)\
                .then_inc(spare_ready, 1)
        MASKS = 2 + ARY + 2

        @block.scalar
        def _(act):
            act.dma_start(params[:, :, :, :], gate_params).then_inc(params_loaded, 16)
            act.dma_start(bias[:, :], conv_bias).then_inc(params_loaded, 16)
            act.dma_start(slope[:, :], prelu_slope.partition_broadcast(P)).then_inc(params_loaded, 16)
            act.wait_ge(masks_ready, 2)
            act.activation(ps_prods[0:2 * N, 0:1], ones8[:, 0:1], ACT.Sigmoid).then_inc(act_summed, 1)
            passes = 1

            def plane_sum(n, ct, func, out, **affine):
                nonlocal passes
                if passes >= 2:
                    act.wait_ge(act_summed, passes - 1)
                act.activation(waste[passes % 2], x_sb[:, ct, :, n * H:(n + 1) * H], func,
                               accum_out=out, **affine).then_inc(act_summed, 1)
                passes += 1

            for ct in range(CT):
                for b in range(2):
                    act.wait_ge(x_loaded[ct][b], 16)
                mine = range(vector_images(ct), N)
                for n in mine:
                    plane_sum(n, ct, ACT.Copy, mean_var[:, n, ct, 0:1], scale=1.0 / PIX)
                act.wait_ge(act_summed, passes)
                act.activation(mean_div[:, mine[0]:N, ct], mean_var[:, mine[0]:N, ct, 0], ACT.Copy,
                               scale=-PIX ** -0.5).then_inc(act_shift_done, 1)
                act.wait_ge(act_shift_done, ct + 1)
                for n in mine:
                    plane_sum(n, ct, ACT.Square, mean_var[:, n, ct, 1:2], scale=PIX ** -0.5,
                              bias=mean_div[:, n, ct:ct + 1])
            w_halves = iter(range(W_LOADS))

            def split_w(count):
                for h in itertools.islice(w_halves, count):
                    act.wait_ge(w_staged[h % 2], 16 * (h // 2 + 1))
                    act.activation(w_half(w_hi, h), stage_half(h), ACT.Copy).then_inc(w_hi_done, 1)

            split_w(W_LOADS // 2)
            for layer in range(LAYERS):
                act.wait_ge(logits_ready, layer + 1)
                act.activation(gate[:, :, :], gate[:, :, :], ACT.Sigmoid).then_inc(gates_ready, 1)
                if layer == 0:
                    split_w(W_LOADS // 2)
            act.wait_ge(params_loaded, 48)
            act.wait_ge(folded, 2)
            with act.Fori(0, STEPS) as i:
                for c in range(2):
                    act.wait_ge(product_done, i * 2 + (c + 1))
                    for r in range(2):
                        half = slice(r * 256, r * 256 + 256)
                        act.wait_ge(column_added, i * 4 + (2 * c + r + 3))
                        act.activation(act_buf[:, half], ps_prod[c][:, half], ACT.Copy).then_inc(raw_copied, 1)
                    for r in range(2):
                        act.wait_ge(transposed, i * 4 + (2 * c + r + 1))
                        for j in range(2):
                            ct = 4 * c + 2 * r + j
                            last = act.activation(act_buf[:, (2 * r + j) * P:(2 * r + j + 1) * P],
                                                  ps_turn[r][:, j * P:(j + 1) * P], ACT.Identity,
                                                  bias=bias[:, ct:ct + 1])
                        last.then_inc(biased, 1)
                        for j in range(2):
                            ct = 4 * c + 2 * r + j
                            last = act.activation(ps_below[:, r * 512 + j * P:r * 512 + (j + 1) * P],
                                                  ps_turn[r][:, j * P:(j + 1) * P], ACT.Relu,
                                                  bias=neg_bias[:, ct:ct + 1], scale=-1.0)
                        last.then_inc(negated, 1)

        @block.tensor
        def _(pe):
            pe.wait_ge(masks_ready, MASKS)
            for layer in range(LAYERS + 1):
                pe.wait_ge(means_asked, layer + 1)
                pe.matmul(ps_group[:, 0:N * CT], group_ones[:, :], stat[:, :, 0, :], start=True, stop=True)\
                    .then_inc(means_given, 1)
                pe.wait_ge(vars_asked, layer + 1)
                pe.matmul(ps_var[:, 0:N * CT], group_ones[:, :], t1[:, 0, :, :].rearrange("p n c -> p (n c)"),
                          start=True, stop=True).then_inc(vars_given, 1)
                if layer == LAYERS:
                    break
                for k in range(ROUNDS):
                    marks = round_marks(k)
                    for s in range(VALUES):
                        if s in PARTS:
                            pe.wait_ge(compared, (layer * ROUNDS + k) * len(PARTS) + PARTS.index(s) + 1)
                        last = pe.matmul(ps_count[:, 0:N * marks], ones_bf[:, :],
                                         less[:, s * N * marks:(s + 1) * N * marks],
                                         start=(s == 0), stop=(s == VALUES - 1))
                    last.then_inc(counted, 1)
                pe.wait_ge(tops_ready, layer + 1)
                pe.matmul(ps_mid[0:2 * N, 0:P], tops[:, :], ident[:, :], start=True, stop=True)\
                    .then_inc(tops_turned, 1)
                pe.wait_ge(median_ready, layer + 1)
                pe.matmul(ps_med[:, 0:N], ones8[:, :], halves[:, :], start=True, stop=True)\
                    .then_inc(median_spread, 1)

            pe.wait_ge(w_lo_done, W_LOADS)
            for _ in range(WARM_UPS):
                pe.matmul(ps_count[:, :], w_hi[:, 0, 0:P], w_hi[:, 0, 0:HALF], start=True, stop=True)

            def unit_products(c, k, between=None):
                w_cols = slice(c * HALF, (c + 1) * HALF)
                pe.matmul(ps_prod[c], s_hi[:, k, :], w_hi[:, k, w_cols], start=(k == 0), stop=False)
                if between:
                    between()
                pe.matmul(ps_prod[c], s_hi[:, k, :], w_lo[:, k, w_cols], start=False, stop=False)
                return pe.matmul(ps_prod[c], s_lo[:, k, :], w_hi[:, k, w_cols],
                                 start=False, stop=(k == CT - 1))

            def turn(r, copies):
                pe.wait_ge(raw_copied, copies)
                for j in range(2):
                    q = 2 * r + j
                    last = pe.transpose(ps_turn[r][:, j * P:(j + 1) * P], act_buf[:, q * P:(q + 1) * P], ident[:, :])
                last.then_inc(transposed, 1)

            def scan_step(i, first):
                for k in range(4):
                    if k % 2 == 0:
                        pe.wait_ge(state_ready, i * 4 + (k // 2 + 1))
                    if k == 1 and not first:
                        unit_products(0, k, lambda: turn(0, i * 4 - 1))
                        turn(1, i * 4)
                    else:
                        unit_products(0, k)
                for k in range(2):
                    unit_products(1, k)
                for k in range(4, CT):
                    if k % 2 == 0:
                        pe.wait_ge(state_ready, i * 4 + (k // 2 + 1))
                    last = unit_products(0, k)
                last.then_inc(product_done, 1)
                unit_products(1, 2)
                unit_products(1, 3, lambda: turn(0, i * 4 + 1)).then_inc(a_state_read, 1)
                turn(1, i * 4 + 2)
                for k in range(4, CT):
                    last = unit_products(1, k)
                last.then_inc(product_done, 1)

            scan_step(0, True)
            scan_step(1, False)
            with pe.Fori(2, STEPS, 2) as i:
                scan_step(i, False)
                scan_step(i + 1, False)
            for r in range(2):
                turn(r, 4 * STEPS - 1 + r)

        @block.vector
        def _(dve):
            links = [0]

            def link(ins):
                links[0] += 1
                ins.then_inc(dve_link, 1)
                dve.wait_ge(dve_link, links[0])

            def rsqrt(out, a, u, v):
                link(dve.tensor_scalar(out.bitcast(i32), a.bitcast(i32), -0.5, float(0x5F3759DF), ALU.mult, ALU.add))
                for _ in range(3):
                    link(dve.tensor_tensor(u, out, out, ALU.mult))
                    link(dve.scalar_tensor_tensor(v, u, -0.5, a, ALU.mult, ALU.mult))
                    link(dve.scalar_tensor_tensor(out, v, 1.5, out, ALU.add, ALU.mult))

            group_var, plane_var = var[:, 0, :, :], var[:, 1, :, :]
            group_rstd, plane_rstd = rstd[:, 0, :, :], rstd[:, 1, :, :]

            for ct in range(CT):
                for b in range(2):
                    dve.wait_ge(x_loaded[ct][b], 16)
                    cols = slice(b * COLS // 2, (b + 1) * COLS // 2)
                    for n in range(vector_images(ct)):
                        last = dve.bn_stats(bn_parts[:, ct, n, b, :], x_sb[:, ct, cols, n * H:(n + 1) * H])
                    if b == 1:
                        link(last)
                        for n in range(vector_images(ct)):
                            dve.bn_aggr(mean_var[:, n, ct, :], bn_parts[:, ct, n, :, :].rearrange("p b s -> p (b s)"))
                    last = dve.tensor_reduce(half_max[:, b, :, ct],
                                             x_sb[:, ct, cols, :].rearrange("p w (n h) -> p n w h", n=N),
                                             AX.XY, ALU.max)
            link(last)
            dve.tensor_tensor(stat[:, :, 1, :], half_max[:, 0, :, :], half_max[:, 1, :, :], ALU.max)
            dve.wait_ge(act_summed, act_passes)
            dve.tensor_copy(stat[:, :, 0, :], mean_var[:, :, :, 0]).then_inc(means_asked, 1)
            dve.tensor_scalar(plane_var, mean_var[:, :, :, 1], PIX / (PIX - 1.0), 1e-30, ALU.mult, ALU.max)
            dve.memset(a_scale[:, :, :], 1.0)
            link(dve.memset(a_shift[:, :, :], 0.0))
            dve.wait_ge(masks_ready, MASKS)
            dve.wait_ge(params_loaded, 48)
            dve.wait_ge(folded, 2 * LAYERS + 2)
            dve.tensor_tensor(fold[:, :], ident[0:2 * N, 0:N], ident[0:2 * N, N:2 * N], ALU.add)

            def group_norm(layer):
                if layer > 0:
                    dve.tensor_tensor(plane_var, stat[:, :, 2, :], stat[:, :, 2, :], ALU.mult)
                dve.wait_ge(means_given, layer + 1)
                means = ps_group[:, 0:N * CT].rearrange("p (n c) -> p n c", n=N)
                link(dve.tensor_tensor(unit[:, :, 0:2, :], stat[:, :, 0:2, :],
                                       means.unsqueeze(2).broadcast_to([P, N, 2, CT]), ALU.subtract))
                link(dve.tensor_tensor(t2[:, 0, :, :], unit[:, :, 0, :], unit[:, :, 0, :], ALU.mult))
                dve.scalar_tensor_tensor(t1[:, 0, :, :], plane_var, (PIX - 1.0) / PIX, t2[:, 0, :, :],
                                         ALU.mult, ALU.add).then_inc(vars_asked, 1)
                if layer > 0:
                    link(dve.tensor_tensor(pull[:, :, :], pull[:, :, :], grow[:, :, :], ALU.mult))
                    dve.tensor_tensor(a_scale[:, :, :], a_scale[:, :, :], scaled[:, :, :], ALU.add)
                    link(dve.tensor_tensor(a_shift[:, :, :], a_shift[:, :, :], pull[:, :, :], ALU.add))
                link(dve.tensor_tensor(pull[:, :, :], a_shift[:, :, :], means, ALU.subtract))
                dve.wait_ge(vars_given, layer + 1)
                link(dve.tensor_scalar(group_var.rearrange("p n c -> p (n c)"), ps_var[:, 0:N * CT],
                                       GN_EPS, None, ALU.add))
                if layer > 0:
                    rsqrt(group_rstd, group_var, t1[:, 0, :, :], t2[:, 0, :, :])
                else:
                    both = "p a n c -> p (a n c)"
                    rsqrt(*(t[:, :, :, :].rearrange(both) for t in (rstd, var, t1, t2)))
                    link(dve.tensor_tensor(stat[:, :, 2, :], plane_var, plane_rstd, ALU.mult))

            def median(layer):
                values = unit[:, :, :, :].rearrange("p n k c -> p n (k c)")

                def place_marks(out, step, start, k):
                    marks = round_marks(k)
                    nth = ticks[:, 0:marks].unsqueeze(1).broadcast_to([P, N, marks])
                    out = out[:, 0:N * marks].rearrange("p (n t) -> p n t", n=N)
                    if isinstance(start, float):
                        link(dve.tensor_scalar(out, nth, step, start, ALU.mult, ALU.add))
                    else:
                        link(dve.scalar_tensor_tensor(out, nth, step, start[:, :].unsqueeze(2)
                                                      .broadcast_to([P, N, marks]), ALU.mult, ALU.add))

                step = SEARCH_WIDTH / ARY
                dve.memset(lo[:, :], SEARCH_LO)
                place_marks(thr, step, SEARCH_LO, 0)
                for k in range(ROUNDS):
                    marks = round_marks(k)
                    last_round = k == ROUNDS - 1
                    below = less[:, 0:VALUES * N * marks].rearrange("p (s n t) -> p n t s", n=N, t=marks)
                    marked = thr[:, 0:N * marks].rearrange("p (n t) -> p n t", n=N)
                    for start, end in zip(PARTS, PARTS[1:] + [VALUES]):
                        vals = slice(start, end)
                        dve.tensor_tensor(below[:, :, :, vals],
                                          values[:, :, vals].unsqueeze(2).broadcast_to([P, N, marks, end - start]),
                                          marked.unsqueeze(3).broadcast_to([P, N, marks, end - start]),
                                          ALU.is_lt).then_inc(compared, 1)
                    if k > 0:
                        link(dve.scalar_tensor_tensor(lo[:, :], cell[:, 0, :], step * ARY, lo[:, :],
                                                      ALU.mult, ALU.add))
                    if not last_round:
                        place_marks(base, step / ARY, lo, k + 1)
                    dve.wait_ge(counted, layer * ROUNDS + k + 1)
                    ranks = 2 if last_round else 1
                    for upper in range(ranks):
                        last = dve.tensor_scalar(few[:, upper, 0:N * marks], ps_count[:, 0:N * marks],
                                                 float(MEDIAN_RANK + upper), None, ALU.is_le)
                    link(last)
                    link(dve.tensor_reduce(cell[:, 0:ranks, :], few[:, 0:ranks, 0:N * marks]
                                           .rearrange("p u (n t) -> p u n t", n=N), AX.X, ALU.add))
                    if not last_round:
                        nxt = round_marks(k + 1)
                        image_thr, image_base = (v[:, 0:N * nxt].rearrange("p (n t) -> p n t", n=N)
                                                 for v in (thr, base))
                        link(dve.scalar_tensor_tensor(image_thr, cell[:, 0, :].unsqueeze(2).broadcast_to([P, N, nxt]),
                                                      step, image_base, ALU.mult, ALU.add))
                        step /= ARY
                link(dve.scalar_tensor_tensor(floors[:, :, :], cell[:, :, :], step,
                                              lo[:, :].unsqueeze(1).broadcast_to([P, 2, N]), ALU.mult, ALU.add))
                each = values.unsqueeze(1).broadcast_to([P, 2, N, VALUES])
                link(dve.tensor_tensor(spread[:, :, :, :], each,
                                       floors[:, :, :].unsqueeze(3).broadcast_to([P, 2, N, VALUES]), ALU.is_lt))
                link(dve.scalar_tensor_tensor(spread[:, :, :, :], spread[:, :, :, :], -BIG, each,
                                              ALU.mult, ALU.subtract))
                dve.tensor_reduce(tops[:, :].rearrange("p (u n) -> p u n", u=2), spread[:, :, :, :], AX.X, ALU.max)\
                    .then_inc(tops_ready, 1)
                dve.wait_ge(tops_turned, layer + 1)
                link(dve.tensor_reduce(middle[:, :], ps_mid[0:2 * N, 0:P], AX.X, ALU.max))
                dve.tensor_scalar(halves[:, :], fold[:, :], middle[:, 0:1], -0.5, ALU.mult, ALU.mult)\
                    .then_inc(median_ready, 1)
                dve.wait_ge(median_spread, layer + 1)

            for layer in range(LAYERS):
                dve.tensor_copy(cube[:, :, NSTAT, :],
                                params[:, layer, NSTAT + 1, :].unsqueeze(1).broadcast_to([P, N, CT]))
                group_norm(layer)
                link(dve.tensor_tensor(unit[:, :, 0:2, :], unit[:, :, 0:2, :],
                                       group_rstd.unsqueeze(2).broadcast_to([P, N, 2, CT]), ALU.mult))
                link(dve.tensor_tensor(unit[:, :, 2, :], stat[:, :, 2, :], group_rstd, ALU.mult))
                median(layer)
                link(dve.tensor_tensor(tall[:, :, :, :].rearrange("p n k c -> p n (k c)"),
                                       unit[:, :, :, :].rearrange("p n k c -> p n (k c)"),
                                       ps_med[:, 0:N].unsqueeze(2).broadcast_to([P, N, VALUES]), ALU.subtract))
                dve.tensor_tensor(cube[:, :, 0:NSTAT, :], tall[:, :, :, :], tall[:, :, :, :], ALU.mult)
                weights = params[:, layer, 0:NSTAT, :].unsqueeze(1).broadcast_to([P, N, NSTAT, CT])
                link(dve.tensor_tensor(tall[:, :, :, :], tall[:, :, :, :], weights, ALU.mult))
                link(dve.tensor_tensor(cube[:, :, 0:NSTAT, :], cube[:, :, 0:NSTAT, :], tall[:, :, :, :], ALU.mult))
                dve.tensor_reduce(gate[:, :, :], cube[:, :, :, :].rearrange("p n k c -> p n c k"), AX.X, ALU.add)\
                    .then_inc(logits_ready, 1)
                dve.wait_ge(gates_ready, layer + 1)
                link(dve.tensor_tensor(tall[:, :, :, :], unit[:, :, :, :],
                                       gate[:, :, :].unsqueeze(2).broadcast_to([P, N, NSTAT, CT]), ALU.mult))
                dve.tensor_tensor(stat[:, :, :, :], stat[:, :, :, :], tall[:, :, :, :], ALU.add)\
                    .then_inc(means_asked, 1)
                link(dve.tensor_tensor(grow[:, :, :], gate[:, :, :], group_rstd, ALU.mult))
                dve.tensor_tensor(scaled[:, :, :], a_scale[:, :, :], grow[:, :, :], ALU.mult)
            group_norm(LAYERS)
            dve.tensor_tensor(g_scale[:, :, :], a_scale[:, :, :], group_rstd, ALU.mult).then_inc(gates_folded, 1)
            link(dve.tensor_tensor(g_shift[:, :, :], pull[:, :, :], group_rstd, ALU.mult))

            def norm_column(w, count):
                dve.tensor_tensor(by_image(column(w)), by_image(column(w)), over_rows(g_scale), ALU.mult)\
                    .then_inc(norm_scaled, 1)
                dve.wait_ge(norm_scaled, count + 1)
                dve.tensor_tensor(by_image(column(w)), by_image(column(w)), over_rows(g_shift), ALU.add)\
                    .then_inc(norm_ready, 1)

            def state_high(w, ct0, nth):
                dve.wait_ge(column_added, nth)
                dve.tensor_scalar(s_hi[:, ct0:ct0 + 2, :], column(w, ct0, 2), 1.0, None, ALU.mult)\
                    .then_inc(hi_written, 1)

            def state_low(w, ct0, nth):
                dve.wait_ge(hi_written, nth)
                dve.tensor_tensor(s_lo[:, ct0:ct0 + 2, :], column(w, ct0, 2),
                                  s_hi[:, ct0:ct0 + 2, :].bitcast(fp32), ALU.subtract).then_inc(state_ready, 1)

            def scan_step(i, w, last=False):
                for c in range(2):
                    def add_above(r):
                        y = act_buf[:, r * 256:(r + 1) * 256].rearrange("p (c m) -> p c m", c=2)
                        col = column(w, 4 * c + 2 * r, 2)
                        dve.wait_ge(biased, i * 4 + (2 * c + r + 1))
                        dve.scalar_tensor_tensor(col, y, 0.0, col, ALU.max, ALU.add).then_inc(above_added, 1)

                    def add_below(r):
                        below = ps_below[:, r * 512:r * 512 + 256].rearrange("p (c m) -> p c m", c=2)
                        col = column(w, 4 * c + 2 * r, 2)
                        dve.wait_ge(above_added, i * 4 + (2 * c + r + 1))
                        dve.wait_ge(negated, i * 4 + (2 * c + r + 1))
                        dve.scalar_tensor_tensor(col, below, neg_slope[:, 0:1], col, ALU.mult, ALU.add)\
                            .then_inc(column_added, 1)

                    nth = i * 4 + (2 * c + 5)
                    add_above(0)
                    add_below(0)
                    add_above(1)
                    if not last:
                        if c == 0:
                            dve.wait_ge(a_state_read, i + 1)
                        state_high(w, 4 * c, nth)
                        state_low(w, 4 * c, nth)
                    add_below(1)
                    if not last:
                        state_high(w, 4 * c + 2, nth + 1)
                        state_low(w, 4 * c + 2, nth + 1)
                    else:
                        half = slice(4 * c, 4 * c + 4)
                        col = column(w, 4 * c, 4)
                        dve.wait_ge(column_added, nth + 1)
                        dve.wait_ge(spare_ready, 1)
                        dve.tensor_tensor(col, col, spare_col[:, half, :], ALU.add).then_inc(out_ready, 1)

            def gated_column(nth):
                dve.wait_ge(x_again, nth * 16)
                dve.tensor_tensor(by_image(stage_col), by_image(stage_col), over_rows(a_scale), ALU.mult)\
                    .then_inc(out_scaled, 1)
                dve.wait_ge(out_scaled, nth)
                dve.tensor_tensor(by_image(stage_col), by_image(stage_col), over_rows(a_shift), ALU.add)\
                    .then_inc(out_shifted, 1)

            def output_column(w, nth, pairs):
                dve.wait_ge(state_ready, pairs)
                dve.wait_ge(out_shifted, nth)
                dve.tensor_tensor(column(w), column(w), stage_col, ALU.add).then_inc(out_ready, 1)

            for q in range(4):
                pair = by_image(column(0, 2 * q, 2))
                scale, shift = (v[:, :, 2 * q:2 * q + 2].rearrange("p n c -> p c n").unsqueeze(3)
                                .broadcast_to([P, 2, N, H]) for v in (g_scale, g_shift))
                link(dve.tensor_tensor(pair, pair, scale, ALU.mult))
                dve.tensor_tensor(pair, pair, shift, ALU.add).then_inc(column_added, 1)
                state_high(0, 2 * q, q + 1)
                state_low(0, 2 * q, q + 1)
            norm_column(1, 0)
            with dve.Fori(0, COLS - 2) as i:
                dve.wait_ge(norm_ready, i + 1)
                scan_step(i, i + 1)
                norm_column(i + 2, i + 1)
            dve.wait_ge(norm_ready, COLS - 1)
            scan_step(COLS - 2, COLS - 1)
            gated_column(1)
            output_column(COLS - 1, 1, 4 * COLS)
            with dve.Fori(0, COLS - 2) as b:
                w = COLS - 2 - b
                dve.compute_val(w)
                scan_step(b + (COLS - 1), w)
                gated_column(b + 2)
                output_column(w, b + 2, (b + COLS) * 4 + 4)
            scan_step(STEPS - 1, 0, last=True)


def kernel(x, L0_conv_cfc_w, L0_conv_bn_w, L0_conv_bn_b, L1_conv_cfc_w, L1_conv_bn_w, L1_conv_bn_b,
           L2_conv_cfc_w, L2_conv_bn_w, L2_conv_bn_b, L3_conv_conv_w, L3_conv_conv_b, L3_conv_prelu_a):
    import numpy as np
    import concourse.bacc as bacc
    from concourse.bass_utils import run_bass_kernel_spmd

    x = np.asarray(x)
    n, c, h, w = x.shape
    p, ct = 128, c // 128
    x_cols = np.ascontiguousarray(x.reshape(n, ct, p, h, w).transpose(2, 1, 4, 0, 3)).reshape(p, ct, w, n * h)
    w_t = np.ascontiguousarray(np.asarray(L3_conv_conv_w)[:, :, 0, 4].T.reshape(ct, p, c).transpose(1, 0, 2))
    by_tile = lambda v: np.asarray(v).reshape(ct, p, -1).transpose(1, 2, 0)
    gates = np.ascontiguousarray(np.stack([
        np.concatenate([by_tile(a), by_tile(b), by_tile(d)], axis=1)
        for a, b, d in ((L0_conv_cfc_w, L0_conv_bn_w, L0_conv_bn_b),
                        (L1_conv_cfc_w, L1_conv_bn_w, L1_conv_bn_b),
                        (L2_conv_cfc_w, L2_conv_bn_w, L2_conv_bn_b))], axis=1))
    bias = np.ascontiguousarray(by_tile(L3_conv_conv_b)[:, 0, :])
    slope = np.asarray(L3_conv_prelu_a).reshape(1)

    nc = bacc.Bacc("TRN2", target_bir_lowering=False, num_devices=1)
    arrays = {"x_cols": x_cols, "w_t": w_t, "gates": gates, "conv_bias": bias, "prelu_slope": slope}
    args = [nc.dram_tensor(name, a.shape, mybir.dt.from_np(a.dtype), kind="ExternalInput").ap()
            for name, a in arrays.items()]
    out = nc.dram_tensor("out_cols", (w, p, ct * n * h), mybir.dt.float32, kind="ExternalOutput").ap()
    gated_norm_and_column_scan_kernel(nc, *args, out)
    got = run_bass_kernel_spmd(nc, [arrays], core_ids=[0]).results[0]["out_cols"]
    return np.ascontiguousarray(got.reshape(w, p, ct, n, h).transpose(3, 2, 1, 4, 0)).reshape(n, c, h, w)
```
